# Optimizing a Trainium2 kernel written in Bass

```python
import numpy as np
import jax
import jax.numpy as jnp

def _softmax(x, axis=-1):
    return jax.nn.softmax(x, axis=axis)

def _gelu(x):
    return jax.nn.gelu(x, approximate=True)

def _silu(x):
    return jax.nn.silu(x)

def _sigmoid(x):
    return jax.nn.sigmoid(x)

def _layernorm(x, axis=-1, eps=1e-05):
    m = jnp.mean(x, axis=axis, keepdims=True)
    v = jnp.var(x, axis=axis, keepdims=True)
    return (x - m) / jnp.sqrt(v + eps)

def _scatter_add(tgt, idx, src, axis=0):
    return tgt.at[idx].add(src)

def _segment_sum(src, seg, n):
    return jax.ops.segment_sum(src, seg, n)
kernel_name = 'mk_seq_postln_d2_jaxref_r4_042bba'

def setup_inputs(seed: int=0):
    np.random.seed(seed)
    _w = jnp.asarray

    def _L0_attn_setup():
        import jax, jax.numpy as jnp
        import numpy as np
        EPS = 1e-06

        def _l2_norm(t):
            inv = 1.0 / jnp.linalg.norm(t, ord=2, axis=-2)
            return t * inv[:, None, :]
        key = jax.random.key(seed)
        ks = jax.random.split(key, 8)
        B, C, D = (16, 512, 256)
        s = 1.0 / np.sqrt(D)
        return {'x': jax.random.normal(ks[0], (B, C, D), dtype=jnp.float32), 'Wq': jax.random.normal(ks[1], (D, D), dtype=jnp.float32) * s, 'bq': jnp.zeros((D,), dtype=jnp.float32), 'Wk': jax.random.normal(ks[2], (D, D), dtype=jnp.float32) * s, 'bk': jnp.zeros((D,), dtype=jnp.float32), 'Wv': jax.random.normal(ks[3], (D, D), dtype=jnp.float32) * s, 'bv': jnp.zeros((D,), dtype=jnp.float32), 'gamma': jax.random.normal(ks[4], (1,), dtype=jnp.float32) * 0.1}
    _L0_attn_in = _L0_attn_setup()

    def _L0_ffn_setup():
        import jax, jax.numpy as jnp
        import numpy as np
        THRESHOLD = 0.1
        key = jax.random.key(seed)
        k1, k2, k3 = jax.random.split(key, 3)
        B, S, D, E = (4, 1024, 256, 8)
        inputs = jax.random.normal(k1, (B, S, D), dtype=jnp.float32)
        gate_w = jax.random.normal(k2, (D, E), dtype=jnp.float32) * 0.02
        gate_b = jnp.zeros((E,), dtype=jnp.float32)
        expert_w = jax.random.normal(k3, (E, D, D), dtype=jnp.float32) * 0.02
        expert_b = jnp.zeros((E, D), dtype=jnp.float32)
        return {'inputs': inputs, 'gate_w': gate_w, 'gate_b': gate_b, 'expert_w': expert_w, 'expert_b': expert_b}
    _L0_ffn_in = _L0_ffn_setup()

    def _L1_attn_setup():
        import jax, jax.numpy as jnp
        import numpy as np
        N_HEADS = 16
        SCALE = 8.0
        key = jax.random.key(seed)
        k1, k2, k3, k4 = jax.random.split(key, 4)
        b, n, d_model, inner = (8, 512, 256, 256)
        x = jax.random.normal(k1, (b, n, d_model), dtype=jnp.float32)
        Wqkv = jax.random.normal(k2, (3 * inner, d_model), dtype=jnp.float32) * (1.0 / np.sqrt(d_model))
        Wproj = jax.random.normal(k3, (d_model, inner), dtype=jnp.float32) * (1.0 / np.sqrt(inner))
        bproj = jax.random.normal(k4, (d_model,), dtype=jnp.float32) * 0.01
        return {'x': x, 'Wqkv': Wqkv, 'Wproj': Wproj, 'bproj': bproj}
    _L1_attn_in = _L1_attn_setup()

    def _L1_ffn_setup():
        import jax, jax.numpy as jnp
        import numpy as np
        CAPACITY_RATIO = 0.75
        key = jax.random.key(seed)
        k1, k2, k3 = jax.random.split(key, 3)
        B, L, D = (4, 2048, 256)
        x = jax.random.normal(k1, (B, L, D), dtype=jnp.float32)
        w_router = jax.random.normal(k2, (D,), dtype=jnp.float32) * 0.02
        w_block = jax.random.normal(k3, (D, D), dtype=jnp.float32) * 0.02
        return {'x': x, 'w_router': w_router, 'w_block': w_block}
    _L1_ffn_in = _L1_ffn_setup()
    _d = {'L0_attn_x': _L0_attn_in['x'], 'L0_attn_Wq': _L0_attn_in['Wq'], 'L0_attn_bq': _L0_attn_in['bq'], 'L0_attn_Wk': _L0_attn_in['Wk'], 'L0_attn_bk': _L0_attn_in['bk'], 'L0_attn_Wv': _L0_attn_in['Wv'], 'L0_attn_bv': _L0_attn_in['bv'], 'L0_attn_gamma': _L0_attn_in['gamma'], 'L0_ffn_gate_w': _L0_ffn_in['gate_w'], 'L0_ffn_gate_b': _L0_ffn_in['gate_b'], 'L0_ffn_expert_w': _L0_ffn_in['expert_w'], 'L0_ffn_expert_b': _L0_ffn_in['expert_b'], 'L1_attn_Wqkv': _L1_attn_in['Wqkv'], 'L1_attn_Wproj': _L1_attn_in['Wproj'], 'L1_attn_bproj': _L1_attn_in['bproj'], 'L1_ffn_w_router': _L1_ffn_in['w_router'], 'L1_ffn_w_block': _L1_ffn_in['w_block']}
    _x0 = _d['L0_attn_x']
    _d['L0_attn_x'] = jax.random.normal(jax.random.fold_in(jax.random.key(seed), 1), (8, 1024, 256), dtype=_x0.dtype)
    del _x0
    return _d

def reference(L0_attn_x, L0_attn_Wq, L0_attn_bq, L0_attn_Wk, L0_attn_bk, L0_attn_Wv, L0_attn_bv, L0_attn_gamma, L0_ffn_gate_w, L0_ffn_gate_b, L0_ffn_expert_w, L0_ffn_expert_b, L1_attn_Wqkv, L1_attn_Wproj, L1_attn_bproj, L1_ffn_w_router, L1_ffn_w_block):

    def _L0_attn_ref(x, Wq, bq, Wk, bk, Wv, bv, gamma):
        import jax, jax.numpy as jnp
        import numpy as np
        EPS = 1e-06

        def _l2_norm(t):
            inv = 1.0 / jnp.linalg.norm(t, ord=2, axis=-2)
            return t * inv[:, None, :]
        B, C, L = x.shape
        Q = x @ Wq.T + bq
        K = x @ Wk.T + bk
        V = x @ Wv.T + bv
        Q = jnp.transpose(_l2_norm(Q), (0, 2, 1))
        K = _l2_norm(K)
        tailor_sum = 1.0 / (L + jnp.einsum('bnc,bc->bn', Q, jnp.sum(K, axis=-1) + EPS))
        value_sum = jnp.sum(V, axis=-1)[:, :, None]
        matrix = jnp.einsum('bmn,bcn->bmc', K, V)
        matrix_sum = value_sum + jnp.einsum('bnm,bmc->bcn', Q, matrix)
        weight_value = matrix_sum * tailor_sum[:, None, :]
        return x + gamma * weight_value

    def _L0_ffn_ref(inputs, gate_w, gate_b, expert_w, expert_b):
        import jax, jax.numpy as jnp
        import numpy as np
        THRESHOLD = 0.1
        d = inputs.shape[-1]
        x = inputs.reshape(-1, d)
        gate_logits = jax.nn.softmax(x @ gate_w + gate_b, axis=-1)
        selected = (gate_logits >= THRESHOLD).astype(x.dtype)
        weights = gate_logits * selected
        wsum = jnp.sum(weights, axis=-1, keepdims=True)
        weights = weights / jnp.where(wsum == 0, jnp.ones_like(wsum), wsum)
        E = expert_w.shape[0]
        out = jnp.zeros((x.shape[0], expert_w.shape[-1]), dtype=x.dtype)
        for e in range(E):
            out = out + weights[:, e:e + 1] * (x @ expert_w[e] + expert_b[e])
        return out.reshape(*inputs.shape[:-1], out.shape[-1])

    def _L1_attn_ref(x, Wqkv, Wproj, bproj):
        import jax, jax.numpy as jnp
        import numpy as np
        N_HEADS = 16
        SCALE = 8.0
        b, n, _ = x.shape
        qkv = jnp.einsum('bnm,fm->bnf', x, Wqkv)
        qkv = qkv.reshape(b, n, N_HEADS, -1)
        dh = qkv.shape[3] // 3
        q, k, v = (qkv[..., :dh], qkv[..., dh:2 * dh], qkv[..., 2 * dh:])
        scores = jnp.einsum('bnhd,bngd->bnhg', q, k) / SCALE
        attn = jax.nn.softmax(scores, axis=-1)
        out = jnp.einsum('bnhg,bngd->bnhd', attn, v)
        out = out.reshape(b, n, -1)
        return jnp.einsum('bni,mi->bnm', out, Wproj) + bproj

    def _L1_ffn_ref(x, w_router, w_block):
        import jax, jax.numpy as jnp
        import numpy as np
        CAPACITY_RATIO = 0.75
        B, L, D = x.shape
        k = max(1, int(L * CAPACITY_RATIO))
        scores = jnp.einsum('bld,d->bl', x, w_router)
        _, top_idx = jax.lax.top_k(scores, k)
        selected = jnp.take_along_axis(x, top_idx[:, :, None], axis=1)
        processed = jax.nn.gelu(jnp.einsum('bkd,de->bke', selected, w_block))
        batch_idx = jnp.arange(B)[:, None]
        out = x.at[batch_idx, top_idx].set(processed)
        return out
    x = L0_attn_x
    x = _layernorm(x + _L0_attn_ref(x, L0_attn_Wq, L0_attn_bq, L0_attn_Wk, L0_attn_bk, L0_attn_Wv, L0_attn_bv, L0_attn_gamma), axis=-1)
    x = _layernorm(x + _L0_ffn_ref(x, L0_ffn_gate_w, L0_ffn_gate_b, L0_ffn_expert_w, L0_ffn_expert_b), axis=-1)
    x = _layernorm(x + _L1_attn_ref(x, L1_attn_Wqkv, L1_attn_Wproj, L1_attn_bproj), axis=-1)
    x = _layernorm(x + _L1_ffn_ref(x, L1_ffn_w_router, L1_ffn_w_block), axis=-1)
    return x

_drawn_inputs = setup_inputs


def setup_inputs(seed=0):
    import zlib

    import numpy as np

    out = dict(_drawn_inputs(seed))
    spreads = {'L0_attn_bq': (0.0, 2.0),
     'L0_attn_bk': (0.0, 2.0),
     'L0_attn_bv': (0.0, 2.0),
     'L0_ffn_gate_b': (0.0, 0.1),
     'L0_ffn_expert_b': (0.0, 0.1)}
    factors = {'L0_attn_Wq': 200.0, 'L0_attn_Wk': 200.0, 'L0_attn_Wv': 200.0, 'L1_attn_bproj': 6.167}
    for name, (base, spread) in spreads.items():
        noise = np.random.default_rng([zlib.crc32(name.encode()), seed]).standard_normal(out[name].shape)
        drawn = base * np.exp(spread * noise) if base else spread * noise
        out[name] = jnp.asarray(drawn.astype(out[name].dtype))
    for name, factor in factors.items():
        out[name] = (out[name] * factor).astype(out[name].dtype)
    return out
```

```python
import concourse.bass as bass
from concourse import mybir
from contextlib import ExitStack


def build_two_layer_postln(nc, x, wqk_t, bqk, wv, bv, gamma, gate_w, gate_b, expert_w, expert_b,
                           wqkv_t, wproj_t, bproj, w_router, w_block, consts, out,
                           scratch_qkv, scratch_o):
    fp32 = mybir.dt.float32
    fp16 = mybir.dt.float16
    ALU = mybir.AluOpType
    ACT = mybir.ActivationFunctionType
    X = mybir.AxisListType.X

    NB, C, D = x.shape
    P = 128
    T = C // P
    TP = T // 2
    KD = D // P
    E = expert_w.shape[1] // D
    H, DH = 16, 16
    NF = 3 * D // P
    KEEP = (C * 3) // 4
    ATT_SCALE = 1.0 / 8.0
    EPS_K = 1e-6
    EPS_LN = 1e-5
    THRESHOLD = 0.1
    WS = 64.0
    HI, LO = 0, 1
    PASSES = ((HI, HI), (HI, LO), (LO, HI))

    A_USES = ["TX0", "TX1", "TX2", "TX3", "GRAM0", "GRAM1", "SROW", "T0", "T1", "TROW", "NORM", "G",
              "IQ", "CSUM", "M", "CB", "AP0", "AP1", "TY0", "AP2", "TY1", "AP3", "TY2", "TY3", "GATE",
              "WT", "BIAS0", "BIAS1", "BIAS2", "BIAS3"]
    B_USES = ["TX0", "TX1", "TX2", "TX3", "F0", "F1", "F2", "F3", "F4", "F5", "F6", "F7", "F8", "F9",
              "F10", "F11", "S0", "S1", "PT0", "S2", "PT1", "S3", "PT2", "PT3", "O0", "O1", "O2", "O3",
              "PR0", "PR1", "TZ0", "PR2", "TZ1", "PR3", "TZ2", "TZ3", "ROUT0", "ROUT1", "SCOL0",
              "SCOL1", "FF0", "FF1", "FF2", "FF3"]
    UA, UB = len(A_USES), len(B_USES)

    ctx = ExitStack()
    with ctx:
        def sb(name, shape, dt=fp32):
            return ctx.enter_context(nc.sbuf_tensor(name, shape, dt))

        def sem(name):
            return ctx.enter_context(nc.semaphore(name))

        blockdiag = sb("blockdiag", [P, P, 2 * P], fp16)
        keys = sb("keys", [P, H, 2 * P], fp16)
        x_in = sb("x_in", [P, T, D])
        xs = sb("xs", [P, T, 2, D], fp16)
        xs_words = xs[:, :, :, :].rearrange("p t l n -> p (t l n)").bitcast(fp32)
        at = sb("at", [P, KD, 2, C], fp16)
        x1 = sb("x1", [P, T, D])
        x2 = x1
        x3 = sb("x3", [P, T, D])
        bt = sb("bt", [P, KD, 2, C], fp16)
        ct = sb("ct", [P, KD, 2, C], fp16)
        stage = sb("stage", [P, 2, 2 * C], fp16)
        prob = sb("prob", [P, 2, 512])
        scores = prob[:, :, :].rearrange("p a n -> p (a n)")
        gelu = sb("gelu", [P, 2, D])
        shared = sb("shared", [P, 8 * D])
        we = sb("we", [P, 2, KD, E * D], fp16)
        wqkv = sb("wqkv", [P, 2, KD, 3 * D], fp16)
        wproj = sb("wproj", [P, 2, KD, D], fp16)
        wblk = sb("wblk", [P, 2, KD, D], fp16)
        wrt = sb("wrt", [P, 2, KD, P], fp16)
        gw = sb("gw", [P, 2, KD, E], fp16)
        wqk = sb("wqk", [P, KD, 2 * D])
        wvs = sb("wvs", [P, KD, D])
        bvr = sb("bvr", [P, KD, P])
        const = sb("const", [P, consts.shape[1]])
        ones = sb("ones", [P, P])
        ones16 = sb("ones16", [P, 1], fp16)
        rows16 = sb("rows16", [P, P], fp16)
        ebd = sb("ebd", [P, 2, T, D], fp16)
        bproj16 = sb("bproj16", [P, D], fp16)
        gb16 = sb("gb16", [P, E], fp16)
        c16 = sb("c16", [P, D], fp16)
        rowtmp = sb("rowtmp", [P, D + E], fp16)
        rowin = bt[:, 0, :, :].rearrange("p l n -> p (l n)").bitcast(fp32)[:, 0:D + E]
        brow = sb("brow", [1, 2 * D])
        eps_row = sb("eps_row", [1, P])
        c_one = sb("c_one", [1, 1])
        gam = sb("gam", [P, 1])
        gram = sb("gram", [P, KD, D + 1])
        srow = sb("srow", [1, D])
        tq = xs_words[:, 0:2 * D].rearrange("p (k n) -> p k n", k=KD)
        trow = xs_words[0:1, 2 * D:4 * D]
        prow = xs_words[0:1, 4 * D:6 * D]
        m16 = xs_words[:, 6 * D:8 * D].bitcast(fp16).rearrange("p (l k n) -> p l k n", l=2, k=KD)
        iq = sb("iq", [P, D])
        gt = sb("gt", [P, D])
        nrm = sb("nrm", [P, 4])
        inv = sb("inv", [P, 4])
        c32 = iq
        gl = sb("gl", [P, T, E])
        ge = sb("ge", [P, T, E])
        gs = sb("gs", [P, T])
        gr = sb("gr", [P, T])
        w32 = sb("w32", [P, T, E])
        wexp = sb("wexp", [P, T, E])
        w16t = sb("w16t", [P, 2, P], fp16)
        half = sb("half", [P, 8])
        stats = sb("stats", [P, 2, 6])
        mvs = [sb(f"mv{i}", [P, 2, 2]) for i in range(2)]
        ves = [sb(f"ve{i}", [P, 2]) for i in range(2)]
        rss = [sb(f"rs{i}", [P, 2]) for i in range(2)]
        smax = sb("smax", [P, 32])
        ssum = sb("ssum", [P, 32])
        srec = sb("srec", [P, 2, 32])
        scol = sb("scol", [P, T])
        rank3 = sb("rank3", [P, T, 3])
        rjunk = gelu[:, :, :].rearrange("p t n -> p (t n)").bitcast(fp16)
        rank = sb("rank", [P, T])
        msel = sb("msel", [P, T])
        mres = sb("mres", [P, T])

        small = sb("small", [P, 2, KD])
        ident = const[:, 0:P]
        lower = const[:, P:2 * P]
        two_i = const[:, 2 * P:2 * P + KD * D]
        prod = shared[:, 0:4 * D].rearrange("p (k n) -> p k n", k=KD)
        gsc = shared[:, 4 * D:6 * D].rearrange("p (k n) -> p k n", k=KD)
        g1 = shared[:, 6 * D:8 * D].rearrange("p (k n) -> p k n", k=KD)
        m32 = shared[:, 0:2 * D]
        diag = shared[:, 2 * D:3 * D].rearrange("p (k n) -> p k n", k=KD)
        den = shared[:, 3 * D:4 * D]
        acc = shared[:, 4 * D:8 * D].rearrange("p (s t n) -> p s t n", s=2, t=2)
        ohl = stage[:, :, :].rearrange("p a n -> p (a n)").rearrange("p (h l n) -> p h l n", h=H, l=2)
        wload = blockdiag[:, :, :].rearrange("p a b -> p (a b)").bitcast(fp32)

        banks = [ctx.enter_context(nc.psum_tensor(f"bank{i}", [P, 512], fp32)) for i in range(8)]
        a_bank, b_bank, m_bank = banks[0:2], banks[2:4], banks[4:8]

        w_loaded = sem("w_loaded")
        w_hi = sem("w_hi")
        w_lo = sem("w_lo")
        init_p = sem("init_p")
        x_ready = [sem(f"x_ready{p}") for p in range(TP)]
        xs_hi = sem("xs_hi")
        xs_lo = sem("xs_lo")
        a_full = sem("a_full")
        a_free = [sem(f"a_free{i}") for i in range(2)]
        b_full = sem("b_full")
        b_free = [sem(f"b_free{i}") for i in range(2)]
        m_full = sem("m_full")
        m_free = [sem(f"m_free{i}") for i in range(4)]
        at_hi = sem("at_hi")
        t_copied = sem("t_copied")
        t_prod = sem("t_prod")
        inv_ready = sem("inv_ready")
        diag_ready = sem("diag_ready")
        g1_ready = sem("g1_ready")
        m32_ready = sem("m32_ready")
        m_hi = sem("m_hi")
        m_lo = sem("m_lo")
        c_hi = sem("c_hi")
        c_lo = sem("c_lo")
        a_mv = sem("a_mv")
        a_rs = sem("a_rs")
        b_mv = sem("b_mv")
        b_rs = sem("b_rs")
        bn_done = [sem("a_bn"), sem("b_bn")]
        ve_sem = [sem("a_ve"), sem("b_ve")]
        gexp = sem("gexp")
        wt_ready = sem("wt_ready")
        wt_hi = sem("wt_hi")
        x2_ready = sem("x2_ready")
        x3_copied = sem("x3_copied")
        bt_hi = sem("bt_hi")
        f_hi = sem("f_hi")
        stored = [sem(f"stored{i}") for i in range(2)]
        qk_loaded = sem("qk_loaded")
        v_loaded = sem("v_loaded")
        p_exp = sem("p_exp")
        p_rec = sem("p_rec")
        p_ready = sem("p_ready")
        pt_hi = sem("pt_hi")
        o_hi = sem("o_hi")
        o_stored = sem("o_stored")
        o_loaded = sem("o_loaded")
        x3_ready = sem("x3_ready")
        y_ready = sem("y_ready")
        out_stored = [sem(f"out_stored{p}") for p in range(TP)]
        waits_held = sem("waits_held")
        ranked = sem("ranked")
        v_step_a = sem("v_step_a")
        v_step_b = sem("v_step_b")
        A_STEPS, B_STEPS = 45, 42

        block = ctx.enter_context(nc.Block())

        def a_use(name):
            return A_USES.index(name)

        def b_use(name):
            return B_USES.index(name)

        def a_ring(name):
            return a_use(name) % 2

        def b_ring(name):
            return b_use(name) % 2

        def a_filled(a, name):
            return a * UA + a_use(name) + 1

        def b_filled(b, name):
            return b * UB + b_use(name) + 1

        def a_read(a, name):
            return a * (UA // 2) + a_use(name) // 2 + 2

        def b_read(b, name):
            return b * (UB // 2) + b_use(name) // 2 + 2

        def a_before(a, name):
            return a_read(a, name) - 1

        def b_before(b, name):
            return b_read(b, name) - 1

        def a_other(a, name, others):
            last = max([a_use(n) for n in others if a_ring(n) != a_ring(name)], default=-2)
            return a * (UA // 2) + last // 2 + 2

        def b_other(b, name, others):
            last = max([b_use(n) for n in others if b_ring(n) != b_ring(name)], default=-2)
            return b * (UB // 2) + last // 2 + 2

        def later(n):
            return not (isinstance(n, int) and n == 0)

        def a_ps(name):
            return a_bank[a_use(name) % 2][:, :]

        def b_ps(name):
            return b_bank[b_use(name) % 2][:, :]

        def pair_cols(buf, part, p):
            return buf[:, :, part, 2 * P * p:2 * P * (p + 1)]

        def f_part(k, part):
            ft, hf = k // 2, k % 2
            if ft < 4:
                return stage[:, ft % 2, :].rearrange("p (r l b c) -> p r l b c", r=T, l=2, b=T)[:, :, part, 4 * hf:4 * hf + 4, :]
            return stage[:, ft % 2, :].rearrange("p (b l n) -> p b l n", b=T, l=2)[:, 4 * hf:4 * hf + 4, part, :]

        def f_psum(k):
            if k // 2 < 4:
                return b_ps(f"F{k}").rearrange("p (b r c) -> p r b c", b=4, r=T)
            return b_ps(f"F{k}").rearrange("p (b n) -> p b n", b=4)

        probs_t = ct[:, :, :, :].rearrange("p k l n -> p (k l n)").rearrange("p (l c m) -> p l c m", l=2, c=16)

        def pt_part(q, part):
            return probs_t[:, part, 4 * q:4 * q + 4, :].rearrange("p c m -> p (c m)")

        def o_part(q, part):
            return ohl[:, :, part, :].rearrange("p h (r c) -> p h r c", c=16)[:, :, :, 4 * q:4 * q + 4]

        def o_psum(q):
            return b_ps(f"O{q}").rearrange("p (c r h) -> p h r c", c=4, r=T)

        class StepCount:
            def __init__(self, per_batch):
                self.per_batch, self.done = per_batch, 0

            def next(self, n):
                self.done += 1
                return n * self.per_batch + (self.done - 1) % self.per_batch + 1

        x_d = x.rearrange("b (t p) d -> b p t d", p=P)
        out_d = out.rearrange("b (t p) d -> b p t d", p=P)
        q_src, k_src, v_src = [scratch_qkv[D * n:D * (n + 1)].rearrange("(h d) (r n) -> h d r n", d=DH, r=T)
                               for n in range(3)]

        def places():
            o = 0
            for n in (E * D, 3 * D, D, D, E):
                yield wload[:, o:o + KD * n].rearrange("p (k n) -> p k n", k=KD)
                o += KD * n
            yield wload[:, o:o + T * D].rearrange("p (t n) -> p t n", t=T)

        we_in, wqkv_in, wproj_in, wblk_in, gw_in, ebd_in = places()
        SPLITS = ((we, we_in, WS), (wqkv, wqkv_in, 1.0), (wproj, wproj_in, 1.0), (wblk, wblk_in, WS),
                  (gw, gw_in, WS), (wrt, small[:, 0, :, None].broadcast_to([P, KD, P]), WS),
                  (ebd, ebd_in, 1.0))
        N_SPLITS = len(SPLITS)
        N_LOADS = 16 + T

        @block.sync
        def _(sp):
            def load(dst, src):
                sp.dma_start(dst, src).then_inc(w_loaded, 16)

            load(const[:, :], consts)
            load(wqk[:, :, :], wqk_t.rearrange("(k p) n -> p k n", p=P))
            load(wvs[:, :, :], wv.rearrange("(k p) n -> p k n", p=P))
            load(small[:, 0, :], w_router)
            load(small[:, 1, :], bv)
            load(brow[:, :], bqk[None, :])
            load(gam[:, :], gamma[None, :].broadcast_to([P, 1]))
            for r in (0, 32):
                load(rowin[r:r + 1, 0:D], bproj[None, :])
                load(rowin[r:r + 1, D:D + E], gate_b[None, :])
            for dst, src in ((we_in, expert_w), (wqkv_in, wqkv_t), (wproj_in, wproj_t),
                             (wblk_in, w_block), (gw_in, gate_w)):
                load(dst, src.rearrange("(k p) n -> p k n", p=P))
            sp.wait_ge(init_p, 1)
            for t in range(T):
                load(ebd_in[t * E:(t + 1) * E, t, :], expert_b)

            def load_x(a, p):
                if later(a):
                    sp.wait_ge(xs_lo, 4 * (a - 1) + p + 1)
                    sp.sem_inc(waits_held, 1)
                    sp.wait_ge(a_full, a_filled(a - 1, f"TX{p}"))
                    sp.sem_inc(waits_held, 1)
                sp.dma_start(x_in[:, 2 * p:2 * p + 2, :], x_d[a][:, 2 * p:2 * p + 2, :])\
                    .then_inc(x_ready[p], 16)

            def a_tx(a, p):
                load_x(a, p)

            def b_f(b, k):
                if k % 2 == 0:
                    return
                ft = k // 2
                sp.wait_ge(b_free[b_ring(f"F{k - 1}")], b_read(b, f"F{k - 1}"))
                sp.sem_inc(waits_held, 1)
                sp.wait_ge(b_free[b_ring(f"F{k}")], b_read(b, f"F{k}"))
                sp.sem_inc(waits_held, 1)
                sp.dma_start(scratch_qkv[P * ft:P * (ft + 1)], stage[:, ft % 2, :]).then_inc(stored[ft % 2], 16)

            def b_loadqk(b):
                for s in range(2):
                    sp.wait_ge(stored[s], 48 * b + 32)
                    sp.sem_inc(waits_held, 1)
                for r in range(T):
                    rows = slice(DH * r, DH * (r + 1))
                    sp.dma_start(blockdiag[rows, H * r:H * (r + 1), :],
                                 q_src[:, :, r, :].rearrange("h d n -> d h n")).then_inc(qk_loaded, 16)
                    sp.dma_start(keys[rows, :, :],
                                 k_src[:, :, r, :].rearrange("h d n -> d h n")).then_inc(qk_loaded, 16)

            def b_loadv(b):
                for s in range(2):
                    sp.wait_ge(stored[s], 48 * b + 48)
                    sp.sem_inc(waits_held, 1)
                sp.wait_ge(b_full, b_filled(b, "S3"))
                for r in range(T):
                    rows = slice(DH * r, DH * (r + 1))
                    sp.dma_start(blockdiag[rows, H * r:H * (r + 1), :],
                                 v_src[:, :, r, :]).then_inc(v_loaded, 16)

            def b_loado(b):
                sp.wait_ge(b_free[b_ring("O2")], b_read(b, "O2"))
                sp.sem_inc(waits_held, 1)
                sp.wait_ge(b_free[b_ring("O3")], b_read(b, "O3"))
                sp.sem_inc(waits_held, 1)
                for r in range(T):
                    sp.dma_start(scratch_o[:, :, r, :].rearrange("h d n -> d h n"),
                                 ohl[DH * r:DH * (r + 1), :, :, :].rearrange("p h l n -> p h (l n)"))\
                        .then_inc(o_stored, 16)
                sp.wait_ge(o_stored, 128 * (b + 1))
                sp.sem_inc(waits_held, 1)
                for ht in range(KD):
                    sp.dma_start(bt[:, ht, :, :].rearrange("p l n -> p (l n)"),
                                 scratch_o[8 * ht:8 * ht + 8].rearrange("h d r n -> (h d) (r n)"))\
                        .then_inc(o_loaded, 16)

            def turn(a, b):
                if a is not None:
                    a_tx(a, 0)
                    a_tx(a, 1)
                    a_tx(a, 2)
                    a_tx(a, 3)
                if b is not None:
                    b_f(b, 0)
                    b_f(b, 1)
                    b_f(b, 2)
                    b_f(b, 3)
                    b_f(b, 4)
                    b_f(b, 5)
                    b_f(b, 6)
                    b_f(b, 7)
                    b_loadqk(b)
                    b_f(b, 8)
                    b_f(b, 9)
                    b_f(b, 10)
                    b_f(b, 11)
                    b_loadv(b)
                    b_loado(b)

            turn(0, None)
            with sp.Fori(1, NB) as i:
                turn(i, i - 1)
            turn(None, NB - 1)
            for s in stored:
                sp.wait_ge(s, 48 * NB)
            sp.wait_ge(o_stored, 16 * T * NB)
            for s in out_stored:
                sp.wait_ge(s, 16 * NB)

        @block.gpsimd
        def _(pool):
            for s in a_free + b_free + m_free:
                pool.sem_inc(s, 1)
            pool.memset(ebd_in, 0.0).then_inc(init_p, 1)
            pool.memset(half[:, :], -0.5)
            pool.memset(rows16[:, :], 0.0)
            pool.memset(bproj16[:, :], 0.0)
            pool.memset(gb16[:, :], 0.0)
            pool.memset(c16[:, :], 0.0)
            pool.memset(ones16[:, :], 1.0)
            pool.memset(w16t[:, :, :], 0.0)
            pool.memset(ones[:, :], 1.0)
            pool.memset(eps_row[:, :], EPS_K)
            pool.memset(c_one[:, :], float(C)).then_inc(init_p, 1)
            pool.wait_ge(init_p, 2)
            pool.memset(rows16[0:1, :], 1.0)
            pool.memset(rows16[32:33, :], 1.0).then_inc(init_p, 1)
            pool.wait_ge(w_hi, N_SPLITS)
            pool.wait_ge(w_lo, N_SPLITS)
            pool.memset(wload, 0.0).then_inc(init_p, 1)

            def ln(n, k, side):
                mv, ve, rs = mvs[side], ves[side], rss[side]
                pool.wait_ge((a_mv, b_mv)[side], 8 * n + k + 1)
                pool.sem_inc(waits_held, 1)
                pool.tensor_scalar(ve[:, :], mv[:, :, 1], EPS_LN, None, ALU.add).then_inc(ve_sem[side], 1)
                pool.wait_ge(ve_sem[side], 8 * n + k + 1)
                pool.tensor_tensor(rs[:, :], ve[:, :], half[:, 0:2], ALU.pow)\
                    .then_inc((a_rs, b_rs)[side], 1)

            def a_norm(a):
                pool.wait_ge(a_free[a_ring("NORM")], a_read(a, "NORM"))
                pool.tensor_tensor(inv[:, :], nrm[:, :], half[:, 0:4], ALU.pow).then_inc(inv_ready, 1)

            def b_tx(b, p):
                pool.wait_ge(x2_ready, 4 * b + p + 1)
                pool.sem_inc(waits_held, 1)
                pool.tensor_copy(x3[:, 2 * p:2 * p + 2, :], x2[:, 2 * p:2 * p + 2, :])\
                    .then_inc(x3_copied, 1)

            def b_s(b, q):
                pool.wait_ge(p_rec, 4 * b + q + 1)
                pr = prob[:, q % 2, :].rearrange("p (a g) -> p a g", g=H)
                pool.tensor_tensor(pr, pr, srec[:, q % 2, :, None].broadcast_to([P, 32, H]), ALU.mult)\
                    .then_inc(p_ready, 1)

            def b_ff(b, p):
                ln(b, 4 + p, 1)
                pool.wait_ge(y_ready, 4 * b + p + 1)
                pool.sem_inc(waits_held, 1)
                pool.dma_start(out_d[b][:, 2 * p:2 * p + 2, :], x3[:, 2 * p:2 * p + 2, :])\
                    .then_inc(out_stored[p], 16)
                if p == TP - 1:
                    for s in out_stored:
                        pool.wait_ge(s, 16 * (b + 1))

            def turn(a, b):
                if b is not None:
                    b_tx(b, 0)
                    b_tx(b, 1)
                    b_tx(b, 2)
                    b_tx(b, 3)
                if a is not None:
                    a_norm(a)
                    ln(a, 0, 0)
                if b is not None:
                    b_s(b, 0)
                if a is not None:
                    ln(a, 1, 0)
                if b is not None:
                    b_s(b, 1)
                if a is not None:
                    ln(a, 2, 0)
                if b is not None:
                    b_s(b, 2)
                if a is not None:
                    ln(a, 3, 0)
                if b is not None:
                    b_s(b, 3)
                if a is not None:
                    ln(a, 4, 0)
                    ln(a, 5, 0)
                if b is not None:
                    ln(b, 0, 1)
                    ln(b, 1, 1)
                if a is not None:
                    ln(a, 6, 0)
                if b is not None:
                    ln(b, 2, 1)
                    ln(b, 3, 1)
                if a is not None:
                    ln(a, 7, 0)
                if b is not None:
                    b_ff(b, 0)
                    b_ff(b, 1)
                    b_ff(b, 2)
                    b_ff(b, 3)

            turn(0, None)
            with pool.Fori(1, NB) as i:
                turn(i, i - 1)
            turn(None, NB - 1)

        @block.scalar
        def _(act):
            def copy(dst, src, scale=1.0):
                return act.activation(dst, src, ACT.Copy, scale=scale)

            act.wait_ge(w_loaded, 16 * N_LOADS)
            act.wait_ge(init_p, 3)
            for w, src, scale in SPLITS:
                copy(w[:, HI, :, :], src, scale).then_inc(w_hi, 1)
            copy(bproj16[0:1, :], rowin[0:1, 0:D])
            copy(gb16[0:1, :], rowin[0:1, D:D + E], WS)
            copy(rowtmp[32:33, 0:D], rowin[32:33, 0:D])
            copy(rowtmp[32:33, D:D + E], rowin[32:33, D:D + E], WS)
            copy(bvr[:, :, :], small[:, 1, :, None].broadcast_to([P, KD, P])).then_inc(w_hi, 1)

            def a_tx(a, p):
                pair = slice(2 * p, 2 * p + 2)
                act.wait_ge(x_ready[p], 16 * (a + 1))
                if later(a):
                    act.wait_ge(a_full, a_filled(a - 1, "GRAM1"))
                copy(xs[:, pair, HI, :], x_in[:, pair, :]).then_inc(xs_hi, 1)
                to_at_hi(a, f"TX{p}", p, p)

            def to_at_hi(a, name, p, n):
                act.wait_ge(a_full, a_filled(a, name))
                if n < 4 and later(a):
                    act.wait_ge(m_full, 32 * (a - 1) + 8 * (p + 1))
                copy(pair_cols(at, HI, p),
                     a_ps(name).rearrange("p (k n) -> p k n", k=KD)).then_inc(at_hi, 1)

            def a_gram(a, m):
                act.wait_ge(a_full, a_filled(a, f"GRAM{m}"))
                copy(gram[:, m, :], a_ps(f"GRAM{m}")[:, 0:D + 1]).then_inc(a_free[a_ring(f"GRAM{m}")], 1)

            def a_srow(a):
                act.wait_ge(a_full, a_filled(a, "SROW"))
                copy(srow[:, :], a_ps("SROW")[0:1, 0:D]).then_inc(a_free[a_ring("SROW")], 1)

            def a_t(a, m):
                act.wait_ge(a_full, a_filled(a, f"T{m}"))
                copy(tq[:, m, :], a_ps(f"T{m}")[:, 0:D]).then_inc(t_copied, 1)

            def a_trow(a):
                act.wait_ge(a_full, a_filled(a, "TROW"))
                copy(trow[:, :], a_ps("TROW")[0:1, :]).then_inc(t_copied, 1)

            def a_iq(a):
                act.wait_ge(a_full, a_filled(a, "IQ"))
                copy(iq[:, :], a_ps("IQ")[:, 0:D]).then_inc(a_free[a_ring("IQ")], 1)

            def a_m(a):
                act.wait_ge(m32_ready, a + 1)
                copy(m16[:, HI, :, :].rearrange("p k n -> p (k n)"), m32).then_inc(m_hi, 1)

            def a_cb(a):
                act.wait_ge(a_free[a_ring("CB")], a_read(a, "CB"))
                copy(c16[0:1, :], c32[0:1, :])
                copy(rowtmp[32:33, 0:D], c32[32:33, :]).then_inc(c_hi, 1)

            def a_gate(a):
                act.wait_ge(a_free[a_ring("GATE")], a_read(a, "GATE"))
                act.activation(ge[:, :, :], gl[:, :, :], ACT.Exp, scale=1.0 / WS).then_inc(gexp, 1)

            def a_wt(a):
                act.wait_ge(a_full, a_filled(a, "WT"))
                copy(w16t[0:T * E, HI, :], a_ps("WT")[0:T * E, 0:P]).then_inc(wt_hi, 1)

            def b_tx(b, p):
                act.wait_ge(b_full, b_filled(b, f"TX{p}"))
                copy(pair_cols(bt, HI, p),
                     b_ps(f"TX{p}").rearrange("p (k n) -> p k n", k=KD)).then_inc(bt_hi, 1)

            def b_f(b, k):
                act.wait_ge(b_full, b_filled(b, f"F{k}"))
                if k // 2 >= 2:
                    act.wait_ge(stored[(k // 2) % 2], 48 * b + 16 * (k // 4))
                copy(f_part(k, HI), f_psum(k)).then_inc(f_hi, 1)

            def b_s(b, q):
                act.wait_ge(b_free[b_ring(f"S{q}")], b_read(b, f"S{q}"))
                act.activation(prob[:, q % 2, :], prob[:, q % 2, :], ACT.Exp, scale=ATT_SCALE)\
                    .then_inc(p_exp, 1)

            def b_pt(b, q):
                act.wait_ge(b_full, b_filled(b, f"PT{q}"))
                copy(pt_part(q, HI), b_ps(f"PT{q}")).then_inc(pt_hi, 1)

            def b_o(b, q):
                act.wait_ge(b_full, b_filled(b, f"O{q}"))
                for s in range(2):
                    act.wait_ge(stored[s], 48 * b + 48)
                copy(o_part(q, HI), o_psum(q)).then_inc(o_hi, 1)

            def b_tz(b, p):
                act.wait_ge(b_full, b_filled(b, f"TZ{p}"))
                copy(pair_cols(ct, HI, p),
                     b_ps(f"TZ{p}").rearrange("p (k n) -> p k n", k=KD)).then_inc(bt_hi, 1)

            def b_rout(b, h):
                act.wait_ge(b_full, b_filled(b, f"ROUT{h}"))
                copy(scores[:, 512 * h:512 * (h + 1)], b_ps(f"ROUT{h}")).then_inc(b_free[b_ring(f"ROUT{h}")], 1)

            def b_ff(b, p):
                act.wait_ge(b_full, b_filled(b, f"FF{p}"))
                act.wait_ge(ranked, b + 1)
                if p > 0:
                    act.wait_ge(y_ready, 4 * b + p)
                act.activation(gelu[:, :, :].rearrange("p t n -> p (t n)"), b_ps(f"FF{p}"),
                                       ACT.Gelu_apprx_tanh, scale=1.0 / WS).then_inc(b_free[b_ring(f"FF{p}")], 1)

            def turn(a, b):
                if a is not None:
                    a_tx(a, 0)
                if b is not None:
                    b_tx(b, 0)
                if a is not None:
                    a_tx(a, 1)
                if b is not None:
                    b_tx(b, 1)
                if a is not None:
                    a_tx(a, 2)
                if b is not None:
                    b_tx(b, 2)
                if a is not None:
                    a_tx(a, 3)
                if b is not None:
                    b_tx(b, 3)
                if a is not None:
                    a_gram(a, 0)
                    a_gram(a, 1)
                if b is not None:
                    b_f(b, 0)
                    b_f(b, 1)
                if a is not None:
                    a_srow(a)
                if b is not None:
                    b_f(b, 2)
                if a is not None:
                    a_t(a, 0)
                    a_t(a, 1)
                    a_trow(a)
                if b is not None:
                    b_f(b, 3)
                    b_f(b, 4)
                    b_f(b, 5)
                if a is not None:
                    a_iq(a)
                if b is not None:
                    b_f(b, 6)
                    b_f(b, 7)
                    b_f(b, 8)
                if a is not None:
                    a_m(a)
                    a_cb(a)
                if b is not None:
                    b_f(b, 9)
                    b_f(b, 10)
                    b_f(b, 11)
                    b_s(b, 0)
                    b_s(b, 1)
                if a is not None:
                    to_at_hi(a, "TY0", 0, 4)
                if b is not None:
                    b_pt(b, 0)
                    b_s(b, 2)
                if a is not None:
                    to_at_hi(a, "TY1", 1, 5)
                if b is not None:
                    b_pt(b, 1)
                    b_s(b, 3)
                if a is not None:
                    to_at_hi(a, "TY2", 2, 6)
                if b is not None:
                    b_pt(b, 2)
                if a is not None:
                    to_at_hi(a, "TY3", 3, 7)
                if b is not None:
                    b_pt(b, 3)
                if a is not None:
                    a_gate(a)
                    a_wt(a)
                if b is not None:
                    b_o(b, 0)
                    b_o(b, 1)
                    b_o(b, 2)
                    b_o(b, 3)
                    b_tz(b, 0)
                    b_tz(b, 1)
                    b_tz(b, 2)
                    b_tz(b, 3)
                    b_rout(b, 0)
                    b_rout(b, 1)
                    b_ff(b, 0)
                    b_ff(b, 1)
                    b_ff(b, 2)
                    b_ff(b, 3)

            turn(0, None)
            with act.Fori(1, NB) as i:
                turn(i, i - 1)
            turn(None, NB - 1)

        @block.vector
        def _(dve):
            def split_lo(dst, src, hi):
                return dve.tensor_tensor(dst, src, hi, ALU.subtract)

            dve.wait_ge(w_loaded, 16 * N_LOADS)
            for n, (w, src, scale) in enumerate(SPLITS):
                dve.wait_ge(w_hi, n + 1)
                dve.scalar_tensor_tensor(out=w[:, LO, :, :], in0=src, scalar=scale, in1=w[:, HI, :, :],
                                         op0=ALU.mult, op1=ALU.subtract).then_inc(w_lo, 1)
            dve.wait_ge(w_hi, N_SPLITS + 1)
            split_lo(bproj16[32:33, :], rowin[32:33, 0:D], rowtmp[32:33, 0:D])
            dve.scalar_tensor_tensor(out=gb16[32:33, :], in0=rowin[32:33, D:D + E], scalar=WS,
                                     in1=rowtmp[32:33, D:D + E], op0=ALU.mult, op1=ALU.subtract)\
                .then_inc(w_lo, 1)

            done_a = StepCount(A_STEPS)
            done_b = StepCount(B_STEPS)

            def transposed_lo(dst, ps, hi):
                return split_lo(dst, ps.rearrange("p (k n) -> p k n", k=KD), hi)

            def pair_stats(srcs, n, k, side):
                for t in range(2):
                    ins = dve.bn_stats(stats[:, t, :], srcs[t])
                ins.then_inc(bn_done[side], 1)
                dve.wait_ge(bn_done[side], 8 * n + k + 1)
                dve.sem_inc(waits_held, 1)
                for t in range(2):
                    ins = dve.bn_aggr(mvs[side][:, t, :], stats[:, t, :])
                ins.then_inc((a_mv, b_mv)[side], 1)

            def pair_norm(dsts, srcs, n, k, side):
                dve.wait_ge((a_rs, b_rs)[side], 8 * n + k + 1)
                for t in range(2):
                    ins = dve.tensor_scalar(dsts[t], srcs[t], mvs[side][:, t, 0:1], rss[side][:, t:t + 1],
                                            ALU.subtract, ALU.mult)
                return ins

            def a_tx(a, p):
                pair = slice(2 * p, 2 * p + 2)
                dve.wait_ge(xs_hi, 4 * a + p + 1)
                split_lo(xs[:, pair, LO, :], x_in[:, pair, :], xs[:, pair, HI, :]).then_inc(xs_lo, 1)
                to_at_lo(a, f"TX{p}", p, p)

            def to_at_lo(a, name, p, n):
                dve.wait_ge(at_hi, 8 * a + n + 1)
                transposed_lo(pair_cols(at, LO, p), a_ps(name), pair_cols(at, HI, p)).then_inc(a_free[a_ring(name)], 1)

            def a_t(a, m):
                dve.wait_ge(t_copied, 3 * a + m + 1)
                dve.tensor_tensor(prod[:, m, :], a_ps(f"T{m}"), wqk[:, m, :], ALU.mult).then_inc(a_free[a_ring(f"T{m}")], 1)

            def a_trow(a):
                dve.wait_ge(t_copied, 3 * a + 3)
                dve.tensor_tensor(prow[:, :], a_ps("TROW")[0:1, :], brow[:, :], ALU.mult).then_inc(a_free[a_ring("TROW")], 1)

            def a_norm(a):
                dve.wait_ge(a_full, a_filled(a, "NORM"))
                dve.tensor_copy(nrm[:, :], a_ps("NORM")[:, 0:4]).then_inc(a_free[a_ring("NORM")], 1)

            def a_g(a):
                dve.wait_ge(a_full, a_filled(a, "G"))
                dve.wait_ge(inv_ready, a + 1)
                for t in range(2):
                    ins = dve.tensor_scalar(diag[:, t, :], ident, inv[:, t:t + 1], None, ALU.mult)
                ins.then_inc(diag_ready, 1)
                for m in range(KD):
                    ins = dve.tensor_scalar(gsc[:, m, :], a_ps("G")[:, D * m:D * (m + 1)],
                                            inv[:, 2 + m:3 + m], None, ALU.mult)
                ins.then_inc(a_free[a_ring("G")], 1)

            def a_csum(a):
                dve.wait_ge(a_free[a_ring("IQ")], a_read(a, "IQ"))
                dve.wait_ge(a_free[a_ring("G")], a_read(a, "G"))
                dve.tensor_tensor(g1, gsc, iq[:, None, :].broadcast_to([P, KD, D]), ALU.mult).then_inc(v_step_a, 1)
                dve.wait_ge(v_step_a, done_a.next(a))
                dve.tensor_scalar(g1, g1, 1.0, None, ALU.add).then_inc(g1_ready, 1)
                dve.wait_ge(a_full, a_filled(a, "CSUM"))
                dve.tensor_tensor(den, a_ps("CSUM")[:, 0:D], iq[:, :], ALU.mult).then_inc(a_free[a_ring("CSUM")], 1)
                dve.wait_ge(a_free[a_ring("CSUM")], a_read(a, "CSUM"))
                dve.tensor_scalar(den, den, float(D), None, ALU.add).then_inc(v_step_a, 1)
                dve.wait_ge(v_step_a, done_a.next(a))
                dve.reciprocal(gt[:, :], den).then_inc(v_step_a, 1)
                dve.wait_ge(v_step_a, done_a.next(a))
                dve.tensor_scalar(gt[:, :], gt[:, :], gam[:, 0:1], None, ALU.mult).then_inc(v_step_a, 1)
                dve.wait_ge(v_step_a, done_a.next(a))

            def a_m(a):
                dve.wait_ge(a_full, a_filled(a, "M"))
                m3 = m32.rearrange("p (k n) -> p k n", k=KD)
                dve.tensor_tensor(m3, a_ps("M").rearrange("p (k n) -> p k n", k=KD),
                                          gt[:, None, :].broadcast_to([P, KD, D]), ALU.mult).then_inc(a_free[a_ring("M")], 1)
                dve.wait_ge(a_free[a_ring("M")], a_read(a, "M"))
                dve.tensor_tensor(m32, m32, two_i, ALU.add).then_inc(m32_ready, 1)
                dve.wait_ge(m_hi, a + 1)
                split_lo(m16[:, LO, :, :].rearrange("p k n -> p (k n)"), m32,
                         m16[:, HI, :, :].rearrange("p k n -> p (k n)")).then_inc(m_lo, 1)

            def a_cb(a):
                dve.wait_ge(a_full, a_filled(a, "CB"))
                dve.tensor_tensor(c32[:, :], a_ps("CB")[:, 0:D], gt[:, :], ALU.mult).then_inc(a_free[a_ring("CB")], 1)
                dve.wait_ge(c_hi, a + 1)
                split_lo(c16[32:33, :], c32[32:33, :], rowtmp[32:33, 0:D]).then_inc(c_lo, 1)

            def a_ap(a, p):
                dve.wait_ge(a_full, a_filled(a, f"AP{p}"))
                src = [a_ps(f"AP{p}")[:, D * t:D * (t + 1)] for t in range(2)]
                pair_stats(src, a, p, 0)
                if later(a):
                    dve.wait_ge(b_full, b_filled(a - 1, "TX3"))
                    dve.wait_ge(x3_copied, 4 * a)
                pair_norm([x1[:, 2 * p + t, :] for t in range(2)], src, a, p, 0).then_inc(a_free[a_ring(f"AP{p}")], 1)

            def a_gate(a):
                dve.wait_ge(a_full, a_filled(a, "GATE"))
                ps = a_ps("GATE")[:, 0:T * E].rearrange("p (t e) -> p t e", e=E)
                bc = lambda v: v[:, :, None].broadcast_to([P, T, E])
                dve.tensor_reduce(gs[:, :], ps, X, ALU.max).then_inc(v_step_a, 1)
                dve.wait_ge(v_step_a, done_a.next(a))
                dve.tensor_tensor(gl[:, :, :], ps, bc(gs), ALU.subtract).then_inc(a_free[a_ring("GATE")], 1)
                dve.wait_ge(gexp, a + 1)
                dve.tensor_reduce(gs[:, :], ge[:, :, :], X, ALU.add).then_inc(v_step_a, 1)
                dve.wait_ge(v_step_a, done_a.next(a))
                dve.reciprocal(gr[:, :], gs[:, :]).then_inc(v_step_a, 1)
                dve.wait_ge(v_step_a, done_a.next(a))
                dve.tensor_tensor(ge[:, :, :], ge[:, :, :], bc(gr), ALU.mult).then_inc(v_step_a, 1)
                dve.wait_ge(v_step_a, done_a.next(a))
                dve.scalar_tensor_tensor(out=gl[:, :, :], in0=ge[:, :, :], scalar=THRESHOLD,
                                              in1=ge[:, :, :], op0=ALU.is_ge, op1=ALU.mult).then_inc(v_step_a, 1)
                dve.wait_ge(v_step_a, done_a.next(a))
                dve.tensor_reduce(gs[:, :], gl[:, :, :], X, ALU.add).then_inc(v_step_a, 1)
                dve.wait_ge(v_step_a, done_a.next(a))
                dve.scalar_tensor_tensor(out=gr[:, :], in0=gs[:, :], scalar=0.0, in1=gs[:, :],
                                              op0=ALU.is_equal, op1=ALU.add).then_inc(v_step_a, 1)
                dve.wait_ge(v_step_a, done_a.next(a))
                dve.reciprocal(gs[:, :], gr[:, :]).then_inc(v_step_a, 1)
                dve.wait_ge(v_step_a, done_a.next(a))
                dve.tensor_tensor(w32[:, :, :], gl[:, :, :], bc(gs), ALU.mult).then_inc(v_step_a, 1)
                dve.wait_ge(v_step_a, done_a.next(a))
                dve.tensor_scalar(wexp[:, :, :], w32[:, :, :], 1.0 / WS, None, ALU.mult)\
                    .then_inc(wt_ready, 1)

            def a_wt(a):
                dve.wait_ge(wt_hi, a + 1)
                split_lo(w16t[0:T * E, LO, :], a_ps("WT")[0:T * E, 0:P], w16t[0:T * E, HI, :]).then_inc(a_free[a_ring("WT")], 1)

            def a_bias(a, p):
                dve.wait_ge(a_full, a_filled(a, f"BIAS{p}"))
                dve.tensor_tensor(acc[:, p % 2, :, :],
                                          a_ps(f"BIAS{p}").rearrange("p (t n) -> p t n", t=2),
                                          x1[:, 2 * p:2 * p + 2, :], ALU.add).then_inc(a_free[a_ring(f"BIAS{p}")], 1)
                dve.wait_ge(a_free[a_ring(f"BIAS{p}")], a_read(a, f"BIAS{p}"))

            def a_moe(a, t):
                dst = acc[:, (t // 2) % 2, t % 2, :]
                dve.wait_ge(wt_ready, a + 1)
                for e in range(E):
                    q = e // 2
                    if e % 2 == 0:
                        dve.wait_ge(m_full, 32 * a + 4 * t + q + 1)
                    ins = dve.scalar_tensor_tensor(out=dst, in0=m_bank[q][:, D * (e % 2):D * (e % 2 + 1)],
                                                   scalar=wexp[:, t, e:e + 1], in1=dst, op0=ALU.mult,
                                                   op1=ALU.add)
                    if e % 2 == 0:
                        ins.then_inc(v_step_a, 1)
                        dve.wait_ge(v_step_a, done_a.next(a))
                    else:
                        ins.then_inc(m_free[q], 1)
                        dve.wait_ge(m_free[q], T * a + t + 2)

            def a_ln2(a, p):
                src = [acc[:, p % 2, t, :] for t in range(2)]
                pair_stats(src, a, 4 + p, 0)
                pair_norm([x2[:, 2 * p + t, :] for t in range(2)], src, a, 4 + p, 0).then_inc(x2_ready, 1)

            def b_tx(b, p):
                dve.wait_ge(bt_hi, 8 * b + p + 1)
                transposed_lo(pair_cols(bt, LO, p), b_ps(f"TX{p}"), pair_cols(bt, HI, p)).then_inc(b_free[b_ring(f"TX{p}")], 1)

            def b_f(b, k):
                dve.wait_ge(f_hi, 12 * b + k + 1)
                split_lo(f_part(k, LO), f_psum(k), f_part(k, HI)).then_inc(b_free[b_ring(f"F{k}")], 1)

            def b_s(b, q):
                dve.wait_ge(b_full, b_filled(b, f"S{q}"))
                ps = b_ps(f"S{q}").rearrange("p (a g) -> p a g", g=H)
                pr = prob[:, q % 2, :].rearrange("p (a g) -> p a g", g=H)
                dve.tensor_reduce(smax[:, :], ps, X, ALU.max).then_inc(v_step_b, 1)
                dve.wait_ge(v_step_b, done_b.next(b))
                dve.tensor_tensor(pr, ps, smax[:, :, None].broadcast_to([P, 32, H]),
                                          ALU.subtract).then_inc(b_free[b_ring(f"S{q}")], 1)
                dve.wait_ge(p_exp, 4 * b + q + 1)
                dve.tensor_reduce(ssum[:, :], pr, X, ALU.add).then_inc(v_step_b, 1)
                dve.wait_ge(v_step_b, done_b.next(b))
                dve.reciprocal(srec[:, q % 2, :], ssum[:, :]).then_inc(p_rec, 1)

            def b_pt(b, q):
                dve.wait_ge(pt_hi, 4 * b + q + 1)
                split_lo(pt_part(q, LO), b_ps(f"PT{q}"), pt_part(q, HI)).then_inc(b_free[b_ring(f"PT{q}")], 1)

            def b_o(b, q):
                dve.wait_ge(o_hi, 4 * b + q + 1)
                split_lo(o_part(q, LO), o_psum(q), o_part(q, HI)).then_inc(b_free[b_ring(f"O{q}")], 1)

            def b_pr(b, p):
                dve.wait_ge(b_full, b_filled(b, f"PR{p}"))
                dve.wait_ge(x3_copied, 4 * b + p + 1)
                pair = x3[:, 2 * p:2 * p + 2, :]
                dve.tensor_tensor(pair, b_ps(f"PR{p}").rearrange("p (t n) -> p t n", t=2),
                                          pair, ALU.add).then_inc(b_free[b_ring(f"PR{p}")], 1)
                dve.wait_ge(b_free[b_ring(f"PR{p}")], b_read(b, f"PR{p}"))
                rows = [x3[:, 2 * p + t, :] for t in range(2)]
                pair_stats(rows, b, p, 1)
                pair_norm(rows, rows, b, p, 1).then_inc(x3_ready, 1)

            def b_tz(b, p):
                dve.wait_ge(bt_hi, 8 * b + 4 + p + 1)
                transposed_lo(pair_cols(ct, LO, p), b_ps(f"TZ{p}"), pair_cols(ct, HI, p)).then_inc(b_free[b_ring(f"TZ{p}")], 1)

            def b_scol(b, h):
                dve.wait_ge(b_full, b_filled(b, f"SCOL{h}"))
                dve.tensor_copy(scol[:, 4 * h:4 * h + 4], b_ps(f"SCOL{h}")[:, 0:4]).then_inc(b_free[b_ring(f"SCOL{h}")], 1)

            def b_rank(b):
                dve.wait_ge(b_free[b_ring("SCOL0")], b_read(b, "SCOL0"))
                dve.wait_ge(b_free[b_ring("SCOL1")], b_read(b, "SCOL1"))
                dve.wait_ge(b_free[b_ring("ROUT1")], b_read(b, "ROUT1"))
                for t in range(T):
                    me = scol[:, t:t + 1]
                    if t == 0:
                        ins = dve.memset(rank3[:, 0, 1:2], 0.0)
                    else:
                        ins = dve.tensor_scalar(rjunk[:, 0:P * t], scores[:, 0:P * t], me, None, ALU.is_ge,
                                                ALU.add, accum_out=rank3[:, t, 1:2])
                    ins.then_inc(v_step_b, 1)
                    dve.wait_ge(v_step_b, done_b.next(b))
                    dve.tensor_scalar(rjunk[:, P * t:C], scores[:, P * t:C], me, None, ALU.is_gt,
                                           ALU.add, accum_out=rank3[:, t, 0:1]).then_inc(v_step_b, 1)
                    dve.wait_ge(v_step_b, done_b.next(b))
                    dve.scalar_tensor_tensor(out=rjunk[:, 0:P], in0=scores[:, P * t:P * (t + 1)],
                                                  scalar=me, in1=lower, op0=ALU.is_equal, op1=ALU.mult,
                                                  accum_out=rank3[:, t, 2:3]).then_inc(v_step_b, 1)
                    dve.wait_ge(v_step_b, done_b.next(b))
                dve.tensor_reduce(rank[:, :], rank3[:, :, :], X, ALU.add).then_inc(v_step_b, 1)
                dve.wait_ge(v_step_b, done_b.next(b))
                dve.tensor_scalar(msel[:, :], rank[:, :], float(KEEP), None, ALU.is_lt).then_inc(v_step_b, 1)
                dve.wait_ge(v_step_b, done_b.next(b))
                dve.tensor_scalar(mres[:, :], msel[:, :], -1.0, 2.0, ALU.mult, ALU.add).then_inc(ranked, 1)
                dve.wait_ge(ranked, b + 1)

            def b_ff(b, p):
                rows = [x3[:, 2 * p + t, :] for t in range(2)]
                for t in range(2):
                    ins = dve.tensor_scalar(rows[t], rows[t], mres[:, 2 * p + t:2 * p + t + 1],
                                            None, ALU.mult)
                ins.then_inc(v_step_b, 1)
                dve.wait_ge(v_step_b, done_b.next(b))
                dve.wait_ge(b_free[b_ring(f"FF{p}")], b_read(b, f"FF{p}"))
                for t in range(2):
                    ins = dve.scalar_tensor_tensor(out=rows[t], in0=gelu[:, t, :],
                                                   scalar=msel[:, 2 * p + t:2 * p + t + 1], in1=rows[t],
                                                   op0=ALU.mult, op1=ALU.add)
                ins.then_inc(v_step_b, 1)
                dve.wait_ge(v_step_b, done_b.next(b))
                pair_stats(rows, b, 4 + p, 1)
                pair_norm(rows, rows, b, 4 + p, 1).then_inc(y_ready, 1)

            def turn(a, b):
                if a is not None:
                    a_tx(a, 0)
                if b is not None:
                    b_tx(b, 0)
                if a is not None:
                    a_tx(a, 1)
                if b is not None:
                    b_tx(b, 1)
                if a is not None:
                    a_tx(a, 2)
                if b is not None:
                    b_tx(b, 2)
                if a is not None:
                    a_tx(a, 3)
                if b is not None:
                    b_tx(b, 3)
                    b_f(b, 0)
                    b_f(b, 1)
                    b_f(b, 2)
                if a is not None:
                    a_t(a, 0)
                    a_t(a, 1)
                    a_trow(a)
                if b is not None:
                    b_f(b, 3)
                if a is not None:
                    a_norm(a)
                    a_g(a)
                if b is not None:
                    b_f(b, 4)
                    b_f(b, 5)
                    b_f(b, 6)
                    b_f(b, 7)
                if a is not None:
                    a_csum(a)
                if b is not None:
                    b_f(b, 8)
                if a is not None:
                    a_m(a)
                    a_cb(a)
                if b is not None:
                    b_f(b, 9)
                    b_f(b, 10)
                    b_f(b, 11)
                if a is not None:
                    a_ap(a, 0)
                if b is not None:
                    b_s(b, 0)
                if a is not None:
                    a_ap(a, 1)
                if b is not None:
                    b_s(b, 1)
                if a is not None:
                    to_at_lo(a, "TY0", 0, 4)
                if b is not None:
                    b_pt(b, 0)
                if a is not None:
                    a_ap(a, 2)
                if b is not None:
                    b_s(b, 2)
                if a is not None:
                    to_at_lo(a, "TY1", 1, 5)
                if b is not None:
                    b_pt(b, 1)
                if a is not None:
                    a_ap(a, 3)
                if b is not None:
                    b_s(b, 3)
                if a is not None:
                    to_at_lo(a, "TY2", 2, 6)
                if b is not None:
                    b_pt(b, 2)
                if a is not None:
                    to_at_lo(a, "TY3", 3, 7)
                if b is not None:
                    b_pt(b, 3)
                if a is not None:
                    a_gate(a)
                    a_wt(a)
                    a_bias(a, 0)
                    a_moe(a, 0)
                    a_moe(a, 1)
                    a_ln2(a, 0)
                if b is not None:
                    b_o(b, 0)
                    b_o(b, 1)
                if a is not None:
                    a_bias(a, 1)
                    a_moe(a, 2)
                if b is not None:
                    b_o(b, 2)
                    b_o(b, 3)
                if a is not None:
                    a_moe(a, 3)
                    a_ln2(a, 1)
                    a_bias(a, 2)
                    a_moe(a, 4)
                if b is not None:
                    b_pr(b, 0)
                    b_pr(b, 1)
                    b_tz(b, 0)
                if a is not None:
                    a_moe(a, 5)
                    a_ln2(a, 2)
                if b is not None:
                    b_pr(b, 2)
                    b_tz(b, 1)
                    b_pr(b, 3)
                    b_tz(b, 2)
                    b_tz(b, 3)
                if a is not None:
                    a_bias(a, 3)
                    a_moe(a, 6)
                if b is not None:
                    b_scol(b, 0)
                    b_scol(b, 1)
                    b_rank(b)
                if a is not None:
                    a_moe(a, 7)
                    a_ln2(a, 3)
                if b is not None:
                    b_ff(b, 0)
                    b_ff(b, 1)
                    b_ff(b, 2)
                    b_ff(b, 3)

            turn(0, None)
            with dve.Fori(1, NB) as i:
                turn(i, i - 1)
            turn(None, NB - 1)
            assert done_a.done % A_STEPS == 0 and done_b.done % B_STEPS == 0

        @block.tensor
        def _(pe):
            def sum_of(dst, terms):
                for n, (lhs, rhs) in enumerate(terms):
                    ins = pe.matmul(dst, lhs, rhs, start=(n == 0), stop=(n == len(terms) - 1))
                return ins

            def split_terms(lhs, rhs):
                return [(lhs(k, i), rhs(k, j)) for k in range(KD) for i, j in PASSES]

            def transpose_pair(ps, src, p):
                for k in range(KD):
                    for t in range(2):
                        ins = pe.transpose(ps[:, 2 * P * k + P * t:2 * P * k + P * (t + 1)],
                                           src[:, 2 * p + t, P * k:P * (k + 1)], ident)
                return ins

            def tok(t):
                return slice(P * t, P * (t + 1))

            pe.wait_ge(init_p, 3)
            pe.wait_ge(w_hi, N_SPLITS + 1)
            pe.wait_ge(w_lo, N_SPLITS + 1)

            def a_tx(a, p):
                pe.wait_ge(x_ready[p], 16 * (a + 1))
                pe.wait_ge(a_free[a_ring(f"TX{p}")], a_before(a, f"TX{p}"))
                transpose_pair(a_ps(f"TX{p}"), x_in, p).then_inc(a_full, 1)

            def a_gram(a, m):
                pe.wait_ge(xs_lo, 4 * (a + 1))
                pe.wait_ge(a_free[a_ring(f"GRAM{m}")], a_before(a, f"GRAM{m}"))
                cols = slice(P * m, P * (m + 1))
                sum_of(a_ps(f"GRAM{m}")[:, 0:D],
                       [(xs[:, t, i, cols], xs[:, t, j, :]) for t in range(T) for i, j in PASSES])
                sum_of(a_ps(f"GRAM{m}")[:, D:D + 1],
                       [(xs[:, t, i, cols], ones16[:, :]) for t in range(T) for i in (HI, LO)])\
                    .then_inc(a_full, 1)

            def a_srow(a):
                pe.wait_ge(a_free[a_ring("SROW")], a_before(a, "SROW"))
                pe.wait_ge(a_free[1 - a_ring("SROW")], a_other(a, "SROW", ("GRAM0", "GRAM1")))
                for m in range(KD):
                    ins = pe.transpose(a_ps("SROW")[0:1, P * m:P * (m + 1)], gram[:, m, D:D + 1], ident)
                ins.then_inc(a_full, 1)

            def a_t(a, m):
                pe.wait_ge(a_free[a_ring(f"T{m}")], a_before(a, f"T{m}"))
                pe.wait_ge(a_free[1 - a_ring(f"T{m}")], a_other(a, f"T{m}", ("SROW",)))
                sum_of(a_ps(f"T{m}"), [(gram[:, k, P * m:P * (m + 1)], wqk[:, k, :]) for k in range(KD)]
                       + [(srow[0:1, P * m:P * (m + 1)], brow[0:1, :])]).then_inc(a_full, 1)

            def a_trow(a):
                pe.wait_ge(a_free[a_ring("TROW")], a_before(a, "TROW"))
                sum_of(a_ps("TROW")[0:1, :], [(gram[:, k, D:D + 1], wqk[:, k, :]) for k in range(KD)]
                       + [(c_one[0:1, 0:1], brow[0:1, :])]).then_inc(a_full, 1)

            def a_norm(a):
                pe.wait_ge(a_free[a_ring("NORM")], a_before(a, "NORM"))
                pe.wait_ge(a_free[1 - a_ring("NORM")], a_other(a, "NORM", ("T0", "T1", "TROW")))
                for c in range(4):
                    ins = sum_of(a_ps("NORM")[:, c:c + 1],
                                 [(prod[:, k, P * c:P * (c + 1)], ones[:, 0:1]) for k in range(KD)]
                                 + [(prow[0:1, P * c:P * (c + 1)], ones[0:1, 0:1])])
                ins.then_inc(a_full, 1)

            def a_g(a):
                pe.wait_ge(t_copied, 3 * a + 3)
                pe.wait_ge(a_free[a_ring("G")], a_before(a, "G"))
                for m in range(KD):
                    cols = slice(D + P * m, D + P * (m + 1))
                    ins = sum_of(a_ps("G")[:, D * m:D * (m + 1)],
                                 [(wqk[:, k, cols], tq[:, k, :]) for k in range(KD)]
                                 + [(brow[0:1, cols], trow[0:1, 0:D])])
                ins.then_inc(a_full, 1)

            def a_iq(a):
                pe.wait_ge(diag_ready, a + 1)
                pe.wait_ge(a_free[a_ring("IQ")], a_before(a, "IQ"))
                pe.matmul(a_ps("IQ")[:, 0:D], ones[:, :], diag.rearrange("p k n -> p (k n)"),
                          start=True, stop=True).then_inc(a_full, 1)

            def a_csum(a):
                pe.wait_ge(a_free[a_ring("CSUM")], a_before(a, "CSUM"))
                pe.wait_ge(a_free[1 - a_ring("CSUM")], a_other(a, "CSUM", ("G",)))
                sum_of(a_ps("CSUM")[:, 0:D], [(ones[:, :], gsc[:, k, :]) for k in range(KD)]
                       + [(eps_row[0:1, :], trow[0:1, 0:D])]).then_inc(a_full, 1)

            def a_m(a):
                pe.wait_ge(g1_ready, a + 1)
                pe.wait_ge(a_free[a_ring("M")], a_before(a, "M"))
                for m in range(KD):
                    ins = sum_of(a_ps("M")[:, D * m:D * (m + 1)],
                                 [(wvs[:, k, P * m:P * (m + 1)], g1[:, k, :]) for k in range(KD)])
                ins.then_inc(a_full, 1)

            def a_cb(a):
                pe.wait_ge(a_free[a_ring("CB")], a_before(a, "CB"))
                sum_of(a_ps("CB")[:, 0:D], [(bvr[:, k, :], g1[:, k, :]) for k in range(KD)])\
                    .then_inc(a_full, 1)

            def a_ap(a, p):
                pe.wait_ge(m_lo, a + 1)
                pe.wait_ge(c_lo, a + 1)
                pe.wait_ge(a_free[a_ring(f"AP{p}")], a_before(a, f"AP{p}"))
                for t in range(2):
                    ins = sum_of(a_ps(f"AP{p}")[:, D * t:D * (t + 1)],
                                 split_terms(lambda k, i: at[:, k, i, tok(2 * p + t)],
                                             lambda k, j: m16[:, j, k, :]) + [(rows16[:, :], c16[:, :])])
                ins.then_inc(a_full, 1)

            def a_ty(a, p):
                pe.wait_ge(a_free[a_ring(f"TY{p}")], a_before(a, f"TY{p}"))
                pe.wait_ge(a_free[1 - a_ring(f"TY{p}")], a_other(a, f"TY{p}", (f"AP{p}",)))
                transpose_pair(a_ps(f"TY{p}"), x1, p).then_inc(a_full, 1)

            def a_gate(a):
                pe.wait_ge(a_free[a_ring("GATE")], a_before(a, "GATE"))
                pe.wait_ge(a_free[1 - a_ring("GATE")], a_other(a, "GATE", [f"TY{p}" for p in range(TP)]))
                for t in range(T):
                    ins = sum_of(a_ps("GATE")[:, E * t:E * (t + 1)],
                                 split_terms(lambda k, i: at[:, k, i, tok(t)],
                                             lambda k, j: gw[:, j, k, :]) + [(rows16[:, :], gb16[:, :])])
                ins.then_inc(a_full, 1)

            def a_wt(a):
                pe.wait_ge(wt_ready, a + 1)
                pe.wait_ge(a_free[a_ring("WT")], a_before(a, "WT"))
                pe.sem_inc(waits_held, 1)
                pe.transpose(a_ps("WT")[0:T * E, 0:P], w32[:, :, :].rearrange("p t e -> p (t e)"), ident)\
                    .then_inc(a_full, 1)

            def a_bias(a, p):
                pe.wait_ge(a_free[a_ring(f"BIAS{p}")], a_before(a, f"BIAS{p}"))
                pe.wait_ge(a_free[1 - a_ring(f"BIAS{p}")], a_other(a, f"BIAS{p}", ("WT",)))
                for t in range(2):
                    ins = sum_of(a_ps(f"BIAS{p}")[:, D * t:D * (t + 1)],
                                 [(w16t[:, i, :], ebd[:, j, 2 * p + t, :]) for i, j in PASSES])
                ins.then_inc(a_full, 1)

            def a_moe(a, t):
                for q in range(4):
                    pe.wait_ge(m_free[q], T * a + t + 1)
                    sum_of(m_bank[q][:, :], split_terms(lambda k, i: at[:, k, i, tok(t)],
                                                        lambda k, j: we[:, j, k, 512 * q:512 * (q + 1)]))\
                        .then_inc(m_full, 1)

            def b_tx(b, p):
                pe.wait_ge(x2_ready, 4 * b + p + 1)
                pe.wait_ge(b_free[b_ring(f"TX{p}")], b_before(b, f"TX{p}"))
                transpose_pair(b_ps(f"TX{p}"), x2, p).then_inc(b_full, 1)

            def b_f(b, k):
                ft, hf = k // 2, k % 2
                pe.wait_ge(b_free[b_ring(f"F{k}")], b_before(b, f"F{k}"))
                pe.wait_ge(b_free[1 - b_ring(f"F{k}")], b_other(b, f"F{k}", (f"TX{2 * hf}", f"TX{2 * hf + 1}")))
                sum_of(b_ps(f"F{k}"), split_terms(lambda k, i: wqkv[:, i, k, P * ft:P * (ft + 1)],
                                                  lambda k, j: bt[:, k, j, 512 * hf:512 * (hf + 1)]))\
                    .then_inc(b_full, 1)

            def b_s(b, q):
                pe.wait_ge(qk_loaded, 32 * T * (b + 1))
                pe.wait_ge(b_free[b_ring(f"S{q}")], b_before(b, f"S{q}"))
                for c in range(4):
                    for g in range(T):
                        token = 16 * g + 4 * q + c
                        n = T * c + g
                        ins = sum_of(b_ps(f"S{q}")[:, H * n:H * (n + 1)],
                                     [(blockdiag[:, :, P * i + token], keys[:, :, P * j + token])
                                      for i, j in PASSES])
                ins.then_inc(b_full, 1)

            def b_pt(b, q):
                pe.wait_ge(p_ready, 4 * b + q + 1)
                pe.wait_ge(b_free[b_ring(f"PT{q}")], b_before(b, f"PT{q}"))
                for c in range(4):
                    ins = pe.transpose(b_ps(f"PT{q}")[:, P * c:P * (c + 1)],
                                       prob[:, q % 2, P * c:P * (c + 1)], ident)
                ins.then_inc(b_full, 1)

            def b_o(b, q):
                pe.wait_ge(v_loaded, 16 * T * (b + 1))
                pe.wait_ge(b_free[b_ring(f"O{q}")], b_before(b, f"O{q}"))
                pe.wait_ge(b_free[1 - b_ring(f"O{q}")], b_other(b, f"O{q}", (f"PT{q}",)))
                for c in range(4):
                    for r in range(T):
                        token = 16 * r + 4 * q + c
                        n = T * c + r
                        ins = sum_of(b_ps(f"O{q}")[:, H * n:H * (n + 1)],
                                     [(blockdiag[:, :, P * i + token],
                                       probs_t[:, j, 4 * q + c, H * r:H * (r + 1)]) for i, j in PASSES])
                ins.then_inc(b_full, 1)

            def b_pr(b, p):
                pe.wait_ge(o_loaded, 16 * KD * (b + 1))
                pe.wait_ge(b_free[b_ring(f"PR{p}")], b_before(b, f"PR{p}"))
                heads = [bt[:, k, :, :].rearrange("p l n -> p (l n)")
                         .rearrange("p (b l n) -> p b l n", b=T, l=2) for k in range(KD)]
                for t in range(2):
                    ins = sum_of(b_ps(f"PR{p}")[:, D * t:D * (t + 1)],
                                 split_terms(lambda k, i: heads[k][:, 2 * p + t, i, :],
                                             lambda k, j: wproj[:, j, k, :])
                                 + [(rows16[:, :], bproj16[:, :])])
                ins.then_inc(b_full, 1)

            def b_tz(b, p):
                pe.wait_ge(x3_ready, 4 * b + p + 1)
                pe.wait_ge(b_free[b_ring(f"TZ{p}")], b_before(b, f"TZ{p}"))
                transpose_pair(b_ps(f"TZ{p}"), x3, p).then_inc(b_full, 1)

            def b_rout(b, h):
                pe.wait_ge(b_free[b_ring(f"ROUT{h}")], b_before(b, f"ROUT{h}"))
                pe.wait_ge(b_free[1 - b_ring(f"ROUT{h}")], b_other(b, f"ROUT{h}", (f"TZ{2 * h}", f"TZ{2 * h + 1}")))
                sum_of(b_ps(f"ROUT{h}"), split_terms(lambda k, i: wrt[:, i, k, :],
                                                     lambda k, j: ct[:, k, j, 512 * h:512 * (h + 1)]))\
                    .then_inc(b_full, 1)

            def b_scol(b, h):
                pe.wait_ge(b_free[b_ring(f"SCOL{h}")], b_before(b, f"SCOL{h}"))
                pe.wait_ge(b_free[1 - b_ring(f"SCOL{h}")], b_other(b, f"SCOL{h}", (f"ROUT{h}",)))
                pe.sem_inc(waits_held, 1)
                for t in range(4):
                    ins = pe.transpose(b_ps(f"SCOL{h}")[:, t:t + 1], scores[0:1, tok(4 * h + t)],
                                       ident[0:1, 0:1])
                ins.then_inc(b_full, 1)

            def b_ff(b, p):
                pe.wait_ge(b_free[b_ring(f"FF{p}")], b_before(b, f"FF{p}"))
                for t in range(2):
                    ins = sum_of(b_ps(f"FF{p}")[:, D * t:D * (t + 1)],
                                 split_terms(lambda k, i: ct[:, k, i, tok(2 * p + t)],
                                             lambda k, j: wblk[:, j, k, :]))
                ins.then_inc(b_full, 1)

            def turn(a, b):
                if a is not None:
                    a_tx(a, 0)
                if b is not None:
                    b_tx(b, 0)
                if a is not None:
                    a_tx(a, 1)
                if b is not None:
                    b_tx(b, 1)
                if a is not None:
                    a_tx(a, 2)
                if b is not None:
                    b_tx(b, 2)
                if a is not None:
                    a_tx(a, 3)
                if b is not None:
                    b_tx(b, 3)
                if a is not None:
                    a_gram(a, 0)
                    a_gram(a, 1)
                if b is not None:
                    b_f(b, 0)
                    b_f(b, 1)
                if a is not None:
                    a_srow(a)
                if b is not None:
                    b_f(b, 2)
                if a is not None:
                    a_t(a, 0)
                    a_t(a, 1)
                    a_trow(a)
                if b is not None:
                    b_f(b, 3)
                if a is not None:
                    a_norm(a)
                    a_g(a)
                if b is not None:
                    b_f(b, 4)
                    b_f(b, 5)
                if a is not None:
                    a_iq(a)
                if b is not None:
                    b_f(b, 6)
                    b_f(b, 7)
                if a is not None:
                    a_csum(a)
                if b is not None:
                    b_f(b, 8)
                if a is not None:
                    a_m(a)
                    a_cb(a)
                if b is not None:
                    b_f(b, 9)
                    b_f(b, 10)
                    b_f(b, 11)
                if a is not None:
                    a_ap(a, 0)
                if b is not None:
                    b_s(b, 0)
                if a is not None:
                    a_ap(a, 1)
                if b is not None:
                    b_s(b, 1)
                if a is not None:
                    a_ty(a, 0)
                if b is not None:
                    b_pt(b, 0)
                if a is not None:
                    a_ap(a, 2)
                if b is not None:
                    b_s(b, 2)
                if a is not None:
                    a_ty(a, 1)
                if b is not None:
                    b_pt(b, 1)
                if a is not None:
                    a_ap(a, 3)
                if b is not None:
                    b_s(b, 3)
                if a is not None:
                    a_ty(a, 2)
                if b is not None:
                    b_pt(b, 2)
                if a is not None:
                    a_ty(a, 3)
                if b is not None:
                    b_pt(b, 3)
                if a is not None:
                    a_gate(a)
                    a_wt(a)
                    a_bias(a, 0)
                    a_moe(a, 0)
                    a_moe(a, 1)
                if b is not None:
                    b_o(b, 0)
                    b_o(b, 1)
                if a is not None:
                    a_bias(a, 1)
                    a_moe(a, 2)
                if b is not None:
                    b_o(b, 2)
                    b_o(b, 3)
                if a is not None:
                    a_moe(a, 3)
                    a_bias(a, 2)
                    a_moe(a, 4)
                if b is not None:
                    b_pr(b, 0)
                    b_pr(b, 1)
                    b_tz(b, 0)
                if a is not None:
                    a_moe(a, 5)
                if b is not None:
                    b_pr(b, 2)
                    b_tz(b, 1)
                    b_pr(b, 3)
                    b_tz(b, 2)
                    b_tz(b, 3)
                if a is not None:
                    a_bias(a, 3)
                    a_moe(a, 6)
                if b is not None:
                    b_rout(b, 0)
                    b_rout(b, 1)
                    b_scol(b, 0)
                    b_scol(b, 1)
                if a is not None:
                    a_moe(a, 7)
                if b is not None:
                    b_ff(b, 0)
                    b_ff(b, 1)
                    b_ff(b, 2)
                    b_ff(b, 3)

            turn(0, None)
            with pe.Fori(1, NB) as i:
                turn(i, i - 1)
            turn(None, NB - 1)


_OUT_SHAPE = (8, 1024, 256)


def kernel(**inputs):
    import numpy as _np
    import concourse.bacc as _bacc
    from concourse import mybir as _mybir
    from concourse.bass_utils import run_bass_kernel_spmd as _run

    a = {k: _np.asarray(v) for k, v in inputs.items()}
    D, HEADS, DH = 256, 16, 16
    wqkv = a["L1_attn_Wqkv"].reshape(HEADS, 3, DH, D).transpose(1, 0, 2, 3).reshape(3 * D, D)
    eye = _np.eye(128, dtype=_np.float32)
    two_i = (2 * _np.eye(D, dtype=_np.float32)).reshape(2, 128, D).transpose(1, 0, 2).reshape(128, 2 * D)
    consts = _np.concatenate([eye, _np.tril(_np.ones((128, 128), _np.float32), -1), two_i], axis=1)
    laid = [
        ("x", a["L0_attn_x"]),
        ("wqk_t", _np.concatenate([a["L0_attn_Wq"].T, a["L0_attn_Wk"].T], axis=1)),
        ("bqk", _np.concatenate([a["L0_attn_bq"], a["L0_attn_bk"]])),
        ("wv", a["L0_attn_Wv"]),
        ("bv", a["L0_attn_bv"].reshape(2, 128).T),
        ("gamma", a["L0_attn_gamma"]),
        ("gate_w", a["L0_ffn_gate_w"]),
        ("gate_b", a["L0_ffn_gate_b"]),
        ("expert_w", a["L0_ffn_expert_w"].transpose(1, 0, 2).reshape(D, -1)),
        ("expert_b", a["L0_ffn_expert_b"]),
        ("wqkv_t", wqkv.T),
        ("wproj_t", a["L1_attn_Wproj"].T),
        ("bproj", a["L1_attn_bproj"]),
        ("w_router", a["L1_ffn_w_router"].reshape(2, 128).T),
        ("w_block", a["L1_ffn_w_block"]),
        ("consts", consts),
    ]
    nc = _bacc.Bacc("TRN2", target_bir_lowering=False, num_devices=1)
    arrays, args = {}, []
    for name, v in laid:
        v = _np.ascontiguousarray(v)
        arrays[f"in_{name}_dram"] = v
        args.append(nc.dram_tensor(f"in_{name}_dram", v.shape, _mybir.dt.from_np(v.dtype),
                                   kind="ExternalInput").ap())
    args.append(nc.dram_tensor("out_0_dram", _OUT_SHAPE, _mybir.dt.float32, kind="ExternalOutput").ap())
    args.append(nc.dram_tensor("scratch_qkv", (3 * D, 2048), _mybir.dt.float16, kind="Internal").ap())
    args.append(nc.dram_tensor("scratch_o", (HEADS, DH, 8, 256), _mybir.dt.float16, kind="Internal").ap())
    build_two_layer_postln(nc, *args)
    r = _run(nc, [arrays], core_ids=[0])
    return r.results[0]["out_0_dram"]
```

```python
import concourse.bass as bass
from concourse import mybir
from contextlib import ExitStack


def build_two_layer_postln(nc, x, wqk_t, bqk, wv, bv, gamma, gate_w, gate_b, expert_w, expert_b,
                           wqkv_t, wproj_t, bproj, w_router, w_block, consts, out,
                           scratch_qkv, scratch_o):
    fp32 = mybir.dt.float32
    fp16 = mybir.dt.float16
    ALU = mybir.AluOpType
    ACT = mybir.ActivationFunctionType
    X = mybir.AxisListType.X

    NB, C, D = x.shape
    P = 128
    T = C // P
    TP = T // 2
    KD = D // P
    E = expert_w.shape[1] // D
    H, DH = 16, 16
    NF = 3 * D // P
    KEEP = (C * 3) // 4
    ATT_SCALE = 1.0 / 8.0
    EPS_K = 1e-6
    EPS_LN = 1e-5
    THRESHOLD = 0.1
    WS = 64.0
    HI, LO = 0, 1
    PASSES = ((HI, HI), (HI, LO), (LO, HI))

    A_USES = ["GRAM0", "GRAM1", "SROW", "TX0", "T0", "T1", "TROW", "TX1", "NORM", "G", "IQ", "CSUM",
              "M", "TX2", "CB", "TX3", "AP0", "AP1", "TY0", "TY1", "AP2", "AP3", "TY2", "TY3", "GATE",
              "WT", "BIAS0", "BIAS1", "BIAS2", "BIAS3"]
    B_USES = ["TX0", "TX1", "TX2", "TX3", "F0", "F1", "F2", "F3", "F4", "F5", "F6", "F7", "F8", "F9",
              "F10", "F11", "S0", "S1", "PT0", "S2", "PT1", "S3", "PT2", "PT3", "O0", "O1", "O2", "O3",
              "PR0", "PR1", "PR2", "PR3", "TZ0", "TZ1", "TZ2", "TZ3", "ROUT0", "ROUT1", "SCOL0",
              "SCOL1"]
    UA, UB = len(A_USES), len(B_USES)

    ctx = ExitStack()
    with ctx:
        def sb(name, shape, dt=fp32):
            return ctx.enter_context(nc.sbuf_tensor(name, shape, dt))

        def sem(name):
            return ctx.enter_context(nc.semaphore(name))

        blockdiag = sb("blockdiag", [P, P, 2 * P], fp16)
        keys = sb("keys", [P, H, 2 * P], fp16)
        x_in = sb("x_in", [P, T, D])
        xs = sb("xs", [P, T, 2, D], fp16)
        xs_words = xs[:, :, :, :].rearrange("p t l n -> p (t l n)").bitcast(fp32)
        at = sb("at", [P, KD, 2, C], fp16)
        x1 = sb("x1", [P, T, D])
        x2 = x1
        x3 = sb("x3", [P, T, D])
        bt = sb("bt", [P, KD, 2, C], fp16)
        ct = sb("ct", [P, KD, 2, C], fp16)
        stage = sb("stage", [P, 2, 2 * C], fp16)
        prob = sb("prob", [P, 2, 512])
        scores = prob[:, :, :].rearrange("p a n -> p (a n)")
        gelu = sb("gelu", [P, 2, D])
        shared = sb("shared", [P, 6 * D])
        part = sb("part", [P, 4, D])
        we = sb("we", [P, 2, KD, E * D], fp16)
        wqkv = sb("wqkv", [P, 2, KD, 3 * D], fp16)
        wproj = sb("wproj", [P, 2, KD, D], fp16)
        wblk = sb("wblk", [P, 2, KD, D], fp16)
        wrt = sb("wrt", [P, 2, KD, P], fp16)
        gw = sb("gw", [P, 2, KD, E], fp16)
        wqk = sb("wqk", [P, KD, 2 * D])
        wvs = sb("wvs", [P, KD, D])
        bvr = sb("bvr", [P, KD, P])
        const = sb("const", [P, consts.shape[1]])
        ones = sb("ones", [P, P])
        ones16 = sb("ones16", [P, 1], fp16)
        rows16 = sb("rows16", [P, P], fp16)
        ebd = sb("ebd", [P, 2, T, D], fp16)
        bproj16 = sb("bproj16", [P, D], fp16)
        gb16 = sb("gb16", [P, E], fp16)
        c16 = sb("c16", [P, D], fp16)
        rowtmp = sb("rowtmp", [P, D + E], fp16)
        rowin = bt[:, 0, :, :].rearrange("p l n -> p (l n)").bitcast(fp32)[:, 0:D + E]
        brow = sb("brow", [1, 2 * D])
        eps_row = rowtmp[0:1, 0:2 * P].bitcast(fp32)
        c_one = sb("c_one", [1, 1])
        gam = sb("gam", [P, 1])
        gram = sb("gram", [P, KD, D + 1])
        tq = xs_words[:, 0:2 * D].rearrange("p (k n) -> p k n", k=KD)
        trow = xs_words[0:1, 2 * D:4 * D]
        prow = xs_words[0:1, 4 * D:6 * D]
        m16 = xs_words[:, 6 * D:8 * D].bitcast(fp16).rearrange("p (l k n) -> p l k n", l=2, k=KD)
        srow = xs_words[0:1, 6 * D:7 * D]
        iq = sb("iq", [P, D])
        gt = sb("gt", [P, D])
        nrm = sb("nrm", [P, 4])
        inv = sb("inv", [P, 4])
        c32 = iq
        gl = sb("gl", [P, T, E])
        ge = sb("ge", [P, T, E])
        gs = sb("gs", [P, T])
        gr = sb("gr", [P, T])
        w32 = sb("w32", [P, T, E])
        wexp = sb("wexp", [P, T, E])
        w16t = sb("w16t", [P, 2, P], fp16)
        half = sb("half", [P, 8])
        stats = [sb(f"stats{i}", [P, 2, 6]) for i in range(2)]
        mv = [sb(f"mv{i}", [P, 8, 2, 2]) for i in range(2)]
        ve = [sb(f"ve{i}", [P, 8, 2]) for i in range(2)]
        rs = [sb(f"rs{i}", [P, 8, 2]) for i in range(2)]
        nm = [sb(f"nm{i}", [P, 8, 2]) for i in range(2)]
        smax = sb("smax", [P, 32])
        ssum = sb("ssum", [P, 32])
        srec = sb("srec", [P, 2, 32])
        scol = sb("scol", [P, T])
        rank3 = sb("rank3", [P, T, 3])
        rjunk = gelu[:, :, :].rearrange("p t n -> p (t n)").bitcast(fp16)
        rjunk2 = sb("rjunk2", [P, P], fp16)
        rank = sb("rank", [P, T])
        msel = sb("msel", [P, T])
        mres = sb("mres", [P, T])

        small = sb("small", [P, 2, KD])
        ident = const[:, 0:P]
        lower = const[:, P:2 * P]
        prod = shared[:, 0:4 * D].rearrange("p (k n) -> p k n", k=KD)
        gsc = shared[:, 0:2 * D].rearrange("p (k n) -> p k n", k=KD)
        g1 = shared[:, 2 * D:4 * D].rearrange("p (k n) -> p k n", k=KD)
        m32 = shared[:, 0:2 * D]
        diag = shared[:, 4 * D:5 * D].rearrange("p (k n) -> p k n", k=KD)
        den = shared[:, 5 * D:6 * D]
        ohl = stage[:, :, :].rearrange("p a n -> p (a n)").rearrange("p (h l n) -> p h l n", h=H, l=2)
        wload = blockdiag[:, :, :].rearrange("p a b -> p (a b)").bitcast(fp32)

        banks = [ctx.enter_context(nc.psum_tensor(f"bank{i}", [P, 512], fp32)) for i in range(8)]
        a_bank, b_bank, m_bank = banks[0:2], banks[2:4], banks[4:8]

        w_loaded = sem("w_loaded")
        w_hi = sem("w_hi")
        w_lo = sem("w_lo")
        init_p = sem("init_p")
        x_ready = [sem(f"x_ready{p}") for p in range(TP)]
        xs_hi = sem("xs_hi")
        xs_lo = sem("xs_lo")
        a_full = sem("a_full")
        a_free = [sem(f"a_free{i}") for i in range(2)]
        b_full = sem("b_full")
        b_free = [sem(f"b_free{i}") for i in range(2)]
        m_full = sem("m_full")
        m_free = [sem(f"m_free{i}") for i in range(4)]
        at_hi = sem("at_hi")
        t_copied = sem("t_copied")
        t_prod = sem("t_prod")
        inv_ready = sem("inv_ready")
        diag_ready = sem("diag_ready")
        g1_ready = sem("g1_ready")
        m32_ready = sem("m32_ready")
        m_hi = sem("m_hi")
        m_lo = sem("m_lo")
        c_hi = sem("c_hi")
        c_lo = sem("c_lo")
        a_mv = sem("a_mv")
        a_rs = sem("a_rs")
        b_mv = sem("b_mv")
        b_rs = sem("b_rs")
        bn_done = [sem("a_bn"), sem("b_bn")]
        ve_sem = [sem("a_ve"), sem("b_ve")]
        dev_sem = [sem("a_dev"), sem("b_dev")]
        m_step = sem("m_step")
        parted = sem("parted")
        part_sum = sem("part_sum")
        chained = sem("chained")
        moe_ready = sem("moe_ready")
        x3_scaled = sem("x3_scaled")
        gexp = sem("gexp")
        wt_ready = sem("wt_ready")
        wt_hi = sem("wt_hi")
        x1_ready = sem("x1_ready")
        x2_ready = sem("x2_ready")
        x3_copied = sem("x3_copied")
        bt_hi = sem("bt_hi")
        f_hi = sem("f_hi")
        stored = [sem(f"stored{i}") for i in range(2)]
        qk_loaded = sem("qk_loaded")
        v_loaded = sem("v_loaded")
        p_exp = sem("p_exp")
        p_rec = sem("p_rec")
        p_ready = sem("p_ready")
        pt_hi = sem("pt_hi")
        o_hi = sem("o_hi")
        o_stored = sem("o_stored")
        o_loaded = sem("o_loaded")
        x3_ready = sem("x3_ready")
        ff_full = sem("ff_full")
        ff_read = sem("ff_read")
        gelu_used = sem("gelu_used")
        y_ready = sem("y_ready")
        out_stored = [sem(f"out_stored{p}") for p in range(TP)]
        waits_held = sem("waits_held")
        ranked = sem("ranked")
        v_step_a = sem("v_step_a")
        v_step_b = sem("v_step_b")
        A_STEPS, B_STEPS = 13, 18

        block = ctx.enter_context(nc.Block())

        def a_use(name):
            return A_USES.index(name)

        def b_use(name):
            return B_USES.index(name)

        def a_ring(name):
            return a_use(name) % 2

        def b_ring(name):
            return b_use(name) % 2

        def a_filled(a, name):
            return a * UA + a_use(name) + 1

        def b_filled(b, name):
            return b * UB + b_use(name) + 1

        def a_read(a, name):
            return a * (UA // 2) + a_use(name) // 2 + 2

        def b_read(b, name):
            return b * (UB // 2) + b_use(name) // 2 + 2

        def a_before(a, name):
            return a_read(a, name) - 1

        def b_before(b, name):
            return b_read(b, name) - 1

        def a_other(a, name, others):
            last = max([a_use(n) for n in others if a_ring(n) != a_ring(name)], default=-2)
            return a * (UA // 2) + last // 2 + 2

        def b_other(b, name, others):
            last = max([b_use(n) for n in others if b_ring(n) != b_ring(name)], default=-2)
            return b * (UB // 2) + last // 2 + 2

        def later(n):
            return not (isinstance(n, int) and n == 0)

        def a_ps(name):
            return a_bank[a_use(name) % 2][:, :]

        def b_ps(name):
            return b_bank[b_use(name) % 2][:, :]

        def pair_cols(buf, part, p):
            return buf[:, :, part, 2 * P * p:2 * P * (p + 1)]

        def f_part(k, part):
            ft, hf = k // 2, k % 2
            if ft < 4:
                return stage[:, ft % 2, :].rearrange("p (r l b c) -> p r l b c", r=T, l=2, b=T)[:, :, part, 4 * hf:4 * hf + 4, :]
            return stage[:, ft % 2, :].rearrange("p (b l n) -> p b l n", b=T, l=2)[:, 4 * hf:4 * hf + 4, part, :]

        def f_psum(k):
            if k // 2 < 4:
                return b_ps(f"F{k}").rearrange("p (b r c) -> p r b c", b=4, r=T)
            return b_ps(f"F{k}").rearrange("p (b n) -> p b n", b=4)

        probs_t = ct[:, :, :, :].rearrange("p k l n -> p (k l n)").rearrange("p (l c m) -> p l c m", l=2, c=16)

        def pt_part(q, part):
            return probs_t[:, part, 4 * q:4 * q + 4, :].rearrange("p c m -> p (c m)")

        def o_part(q, part):
            return ohl[:, :, part, :].rearrange("p h (r c) -> p h r c", c=16)[:, :, :, 4 * q:4 * q + 4]

        def o_psum(q):
            return b_ps(f"O{q}").rearrange("p (c r h) -> p h r c", c=4, r=T)

        class StepCount:
            def __init__(self, per_batch):
                self.per_batch, self.done = per_batch, 0

            def next(self, n):
                self.done += 1
                return n * self.per_batch + (self.done - 1) % self.per_batch + 1

        x_d = x.rearrange("b (t p) d -> b p t d", p=P)
        out_d = out.rearrange("b (t p) d -> b p t d", p=P)
        q_src, k_src, v_src = [scratch_qkv[D * n:D * (n + 1)].rearrange("(h d) (r n) -> h d r n", d=DH, r=T)
                               for n in range(3)]

        def places():
            o = 0
            for n in (E * D, 3 * D, D, D, E):
                yield wload[:, o:o + KD * n].rearrange("p (k n) -> p k n", k=KD)
                o += KD * n
            yield wload[:, o:o + T * D].rearrange("p (t n) -> p t n", t=T)

        we_in, wqkv_in, wproj_in, wblk_in, gw_in, ebd_in = places()
        SPLITS = ((we, we_in, WS), (wqkv, wqkv_in, 1.0), (wproj, wproj_in, 1.0), (wblk, wblk_in, WS),
                  (gw, gw_in, WS), (wrt, small[:, 0, :, None].broadcast_to([P, KD, P]), WS),
                  (ebd, ebd_in, 1.0))
        N_SPLITS = len(SPLITS)
        N_LOADS = 16 + T

        @block.sync
        def _(sp):
            def load(dst, src):
                sp.dma_start(dst, src).then_inc(w_loaded, 16)

            load(const[:, :], consts)
            load(wqk[:, :, :], wqk_t.rearrange("(k p) n -> p k n", p=P))
            load(wvs[:, :, :], wv.rearrange("(k p) n -> p k n", p=P))
            load(small[:, 0, :], w_router)
            load(small[:, 1, :], bv)
            load(brow[:, :], bqk[None, :])
            load(gam[:, :], gamma[None, :].broadcast_to([P, 1]))
            for r in (0, 32):
                load(rowin[r:r + 1, 0:D], bproj[None, :])
                load(rowin[r:r + 1, D:D + E], gate_b[None, :])
            for dst, src in ((we_in, expert_w), (wqkv_in, wqkv_t), (wproj_in, wproj_t),
                             (wblk_in, w_block), (gw_in, gate_w)):
                load(dst, src.rearrange("(k p) n -> p k n", p=P))
            sp.wait_ge(init_p, 1)
            for t in range(T):
                load(ebd_in[t * E:(t + 1) * E, t, :], expert_b)

            def load_x(a, p):
                if later(a):
                    sp.wait_ge(xs_lo, 4 * (a - 1) + p + 1)
                    sp.sem_inc(waits_held, 1)
                    sp.wait_ge(a_full, a_filled(a - 1, f"TX{p}"))
                    sp.sem_inc(waits_held, 1)
                sp.dma_start(x_in[:, 2 * p:2 * p + 2, :], x_d[a][:, 2 * p:2 * p + 2, :])\
                    .then_inc(x_ready[p], 16)

            def b_f(b, k):
                if k % 2 == 0:
                    return
                ft = k // 2
                sp.wait_ge(b_free[b_ring(f"F{k - 1}")], b_read(b, f"F{k - 1}"))
                sp.sem_inc(waits_held, 1)
                sp.wait_ge(b_free[b_ring(f"F{k}")], b_read(b, f"F{k}"))
                sp.sem_inc(waits_held, 1)
                sp.dma_start(scratch_qkv[P * ft:P * (ft + 1)], stage[:, ft % 2, :]).then_inc(stored[ft % 2], 16)

            def b_loadqk(b):
                for s in range(2):
                    sp.wait_ge(stored[s], 48 * b + 32)
                    sp.sem_inc(waits_held, 1)
                for r in range(T):
                    rows = slice(DH * r, DH * (r + 1))
                    sp.dma_start(blockdiag[rows, H * r:H * (r + 1), :],
                                 q_src[:, :, r, :].rearrange("h d n -> d h n")).then_inc(qk_loaded, 16)
                    sp.dma_start(keys[rows, :, :],
                                 k_src[:, :, r, :].rearrange("h d n -> d h n")).then_inc(qk_loaded, 16)

            def b_loadv(b):
                for s in range(2):
                    sp.wait_ge(stored[s], 48 * b + 48)
                    sp.sem_inc(waits_held, 1)
                sp.wait_ge(b_full, b_filled(b, "S3"))
                for r in range(T):
                    rows = slice(DH * r, DH * (r + 1))
                    sp.dma_start(blockdiag[rows, H * r:H * (r + 1), :],
                                 v_src[:, :, r, :]).then_inc(v_loaded, 16)

            def b_loado(b):
                sp.wait_ge(b_free[b_ring("O2")], b_read(b, "O2"))
                sp.sem_inc(waits_held, 1)
                sp.wait_ge(b_free[b_ring("O3")], b_read(b, "O3"))
                sp.sem_inc(waits_held, 1)
                for r in range(T):
                    sp.dma_start(scratch_o[:, :, r, :].rearrange("h d n -> d h n"),
                                 ohl[DH * r:DH * (r + 1), :, :, :].rearrange("p h l n -> p h (l n)"))\
                        .then_inc(o_stored, 16)
                sp.wait_ge(o_stored, 128 * (b + 1))
                sp.sem_inc(waits_held, 1)
                for ht in range(KD):
                    sp.dma_start(bt[:, ht, :, :].rearrange("p l n -> p (l n)"),
                                 scratch_o[8 * ht:8 * ht + 8].rearrange("h d r n -> (h d) (r n)"))\
                        .then_inc(o_loaded, 16)

            def turn(a, b, c):
                if a is not None:
                    load_x(a, 0)
                    load_x(a, 1)
                    load_x(a, 2)
                    load_x(a, 3)
                if c is not None:
                    b_loadv(c)
                    b_loado(c)
                if b is not None:
                    b_f(b, 1)
                    b_f(b, 3)
                    b_f(b, 5)
                    b_f(b, 7)
                    b_loadqk(b)
                    b_f(b, 9)
                    b_f(b, 11)

            turn(0, None, None)
            turn(1, 0, None)
            with sp.Fori(2, NB) as i:
                turn(i, i - 1, i - 2)
            turn(None, NB - 1, NB - 2)
            turn(None, None, NB - 1)
            for s in stored:
                sp.wait_ge(s, 48 * NB)
            sp.wait_ge(o_stored, 16 * T * NB)
            for s in out_stored:
                sp.wait_ge(s, 16 * NB)

        @block.gpsimd
        def _(pool):
            for s in a_free + b_free + m_free:
                pool.sem_inc(s, 1)
            pool.sem_inc(ff_read, 4)
            pool.memset(ebd_in, 0.0).then_inc(init_p, 1)
            pool.memset(half[:, :], -0.5)
            pool.memset(rows16[:, :], 0.0)
            pool.memset(bproj16[:, :], 0.0)
            pool.memset(gb16[:, :], 0.0)
            pool.memset(c16[:, :], 0.0)
            pool.memset(ones16[:, :], 1.0)
            pool.memset(w16t[:, :, :], 0.0)
            pool.memset(ones[:, :], 1.0)
            pool.memset(eps_row[:, :], EPS_K)
            pool.memset(c_one[:, :], float(C)).then_inc(init_p, 1)
            pool.wait_ge(init_p, 2)
            pool.memset(rows16[0:1, :], 1.0)
            pool.memset(rows16[32:33, :], 1.0).then_inc(init_p, 1)
            pool.wait_ge(w_hi, N_SPLITS)
            pool.wait_ge(w_lo, N_SPLITS)
            pool.memset(wload, 0.0).then_inc(init_p, 1)

            def ln(n, k, side):
                pool.wait_ge((a_mv, b_mv)[side], 8 * n + k + 1)
                pool.sem_inc(waits_held, 1)
                pool.tensor_scalar(nm[side][:, k, :], mv[side][:, k, :, 0], -1.0, None, ALU.mult)
                pool.tensor_scalar(ve[side][:, k, :], mv[side][:, k, :, 1], EPS_LN, None, ALU.add)\
                    .then_inc(ve_sem[side], 1)
                pool.wait_ge(ve_sem[side], 8 * n + k + 1)
                pool.tensor_tensor(rs[side][:, k, :], ve[side][:, k, :], half[:, 0:2], ALU.pow)\
                    .then_inc(dev_sem[side], 1)
                pool.wait_ge(dev_sem[side], 8 * n + k + 1)
                pool.tensor_tensor(nm[side][:, k, :], nm[side][:, k, :], rs[side][:, k, :], ALU.mult)\
                    .then_inc((a_rs, b_rs)[side], 1)

            def a_xs(a, p):
                pair = slice(2 * p, 2 * p + 2)
                pool.wait_ge(xs_hi, 4 * a + p + 1)
                pool.tensor_tensor(xs[:, pair, LO, :], x_in[:, pair, :], xs[:, pair, HI, :], ALU.subtract)\
                    .then_inc(xs_lo, 1)

            def a_sum(a, t):
                pool.wait_ge(parted, T * a + t + 1)
                pool.tensor_tensor(part[:, 0:2, :], part[:, 0:2, :], part[:, 2:4, :], ALU.add)\
                    .then_inc(part_sum, 1)
                pool.wait_ge(part_sum, 2 * T * a + 2 * t + 1)
                pool.tensor_tensor(part[:, 0, :], part[:, 0, :], part[:, 1, :], ALU.add)\
                    .then_inc(part_sum, 1)
                pool.wait_ge(part_sum, 2 * T * a + 2 * t + 2)
                pool.wait_ge(chained, T * a + t + 1)
                pool.tensor_tensor(x1[:, t, :], x1[:, t, :], part[:, 0, :], ALU.add)\
                    .then_inc(moe_ready, 1)

            def a_norm(a):
                pool.wait_ge(a_free[a_ring("NORM")], a_read(a, "NORM"))
                pool.tensor_tensor(inv[:, :], nrm[:, :], half[:, 0:4], ALU.pow).then_inc(inv_ready, 1)

            def b_copy(b, p):
                pool.wait_ge(x2_ready, 4 * b + p + 1)
                pool.sem_inc(waits_held, 1)
                if later(b):
                    pool.wait_ge(out_stored[p], 16 * b)
                    pool.sem_inc(waits_held, 1)
                pool.tensor_copy(x3[:, 2 * p:2 * p + 2, :], x2[:, 2 * p:2 * p + 2, :])\
                    .then_inc(x3_copied, 1)

            def b_s(b, q):
                pool.wait_ge(p_rec, 4 * b + q + 1)
                pr = prob[:, q % 2, :].rearrange("p (a g) -> p a g", g=H)
                pool.tensor_tensor(pr, pr, srec[:, q % 2, :, None].broadcast_to([P, 32, H]), ALU.mult)\
                    .then_inc(p_ready, 1)

            def b_store(b, p):
                pool.wait_ge(y_ready, 4 * b + p + 1)
                pool.sem_inc(waits_held, 1)
                pool.dma_start(out_d[b][:, 2 * p:2 * p + 2, :], x3[:, 2 * p:2 * p + 2, :])\
                    .then_inc(out_stored[p], 16)

            def turn(a, b, c):
                if a is not None:
                    a_xs(a, 0)
                    a_xs(a, 1)
                if c is not None:
                    b_s(c, 0)
                    b_s(c, 1)
                if a is not None:
                    a_xs(a, 2)
                if b is not None:
                    a_sum(b, 0)
                if c is not None:
                    b_s(c, 2)
                if a is not None:
                    a_xs(a, 3)
                if b is not None:
                    a_sum(b, 1)
                if c is not None:
                    b_s(c, 3)
                if b is not None:
                    ln(b, 4, 0)
                    a_sum(b, 2)
                    a_sum(b, 3)
                if c is not None:
                    ln(c, 0, 1)
                    ln(c, 1, 1)
                    ln(c, 2, 1)
                    ln(c, 3, 1)
                if b is not None:
                    ln(b, 5, 0)
                    a_sum(b, 4)
                if a is not None:
                    a_norm(a)
                if b is not None:
                    a_sum(b, 5)
                    ln(b, 6, 0)
                    a_sum(b, 6)
                    a_sum(b, 7)
                if c is not None:
                    ln(c, 4, 1)
                if b is not None:
                    ln(b, 7, 0)
                if c is not None:
                    ln(c, 5, 1)
                    b_store(c, 0)
                if a is not None:
                    ln(a, 0, 0)
                if c is not None:
                    b_store(c, 1)
                if b is not None:
                    b_copy(b, 0)
                if a is not None:
                    ln(a, 1, 0)
                if c is not None:
                    ln(c, 6, 1)
                if b is not None:
                    b_copy(b, 1)
                if c is not None:
                    ln(c, 7, 1)
                    b_store(c, 2)
                    b_store(c, 3)
                if b is not None:
                    b_copy(b, 2)
                if a is not None:
                    ln(a, 2, 0)
                if b is not None:
                    b_copy(b, 3)
                if a is not None:
                    ln(a, 3, 0)

            turn(0, None, None)
            turn(1, 0, None)
            with pool.Fori(2, NB) as i:
                turn(i, i - 1, i - 2)
            turn(None, NB - 1, NB - 2)
            turn(None, None, NB - 1)

        @block.scalar
        def _(act):
            def copy(dst, src, scale=1.0):
                return act.activation(dst, src, ACT.Copy, scale=scale)

            act.wait_ge(w_loaded, 16 * N_LOADS)
            act.wait_ge(init_p, 3)
            for w, src, scale in SPLITS:
                copy(w[:, HI, :, :], src, scale).then_inc(w_hi, 1)
            copy(bproj16[0:1, :], rowin[0:1, 0:D])
            copy(gb16[0:1, :], rowin[0:1, D:D + E], WS)
            copy(rowtmp[32:33, 0:D], rowin[32:33, 0:D])
            copy(rowtmp[32:33, D:D + E], rowin[32:33, D:D + E], WS)
            copy(bvr[:, :, :], small[:, 1, :, None].broadcast_to([P, KD, P])).then_inc(w_hi, 1)

            def a_xs(a, p):
                pair = slice(2 * p, 2 * p + 2)
                act.wait_ge(x_ready[p], 16 * (a + 1))
                if later(a):
                    act.wait_ge(a_full, a_filled(a - 1, "GRAM1"))
                copy(xs[:, pair, HI, :], x_in[:, pair, :]).then_inc(xs_hi, 1)

            def to_at_hi(a, name, p, n):
                act.wait_ge(a_full, a_filled(a, name))
                if n < 4 and later(a):
                    act.wait_ge(m_full, 32 * (a - 1) + 8 * (p + 1))
                copy(pair_cols(at, HI, p),
                     a_ps(name).rearrange("p (k n) -> p k n", k=KD)).then_inc(at_hi, 1)

            def a_gram(a, m):
                act.wait_ge(a_full, a_filled(a, f"GRAM{m}"))
                copy(gram[:, m, :], a_ps(f"GRAM{m}")[:, 0:D + 1]).then_inc(a_free[a_ring(f"GRAM{m}")], 1)

            def a_srow(a):
                act.wait_ge(a_full, a_filled(a, "SROW"))
                copy(srow[:, :], a_ps("SROW")[0:1, 0:D]).then_inc(a_free[a_ring("SROW")], 1)

            def a_t(a, m):
                act.wait_ge(a_full, a_filled(a, f"T{m}"))
                copy(tq[:, m, :], a_ps(f"T{m}")[:, 0:D]).then_inc(t_copied, 1)

            def a_trow(a):
                act.wait_ge(a_full, a_filled(a, "TROW"))
                copy(trow[:, :], a_ps("TROW")[0:1, :]).then_inc(t_copied, 1)

            def a_iq(a):
                act.wait_ge(a_full, a_filled(a, "IQ"))
                copy(iq[:, :], a_ps("IQ")[:, 0:D]).then_inc(a_free[a_ring("IQ")], 1)

            def a_m(a):
                act.wait_ge(m32_ready, a + 1)
                copy(m16[:, HI, :, :].rearrange("p k n -> p (k n)"), m32).then_inc(m_hi, 1)

            def a_cb(a):
                act.wait_ge(a_free[a_ring("CB")], a_read(a, "CB"))
                copy(c16[0:1, :], c32[0:1, :])
                copy(rowtmp[32:33, 0:D], c32[32:33, :]).then_inc(c_hi, 1)

            def a_gate(a):
                act.wait_ge(a_free[a_ring("GATE")], a_read(a, "GATE"))
                act.activation(ge[:, :, :], gl[:, :, :], ACT.Exp, scale=1.0 / WS).then_inc(gexp, 1)

            def a_wt(a):
                act.wait_ge(a_full, a_filled(a, "WT"))
                copy(w16t[0:T * E, HI, :], a_ps("WT")[0:T * E, 0:P]).then_inc(wt_hi, 1)

            def b_tx(b, p):
                act.wait_ge(b_full, b_filled(b, f"TX{p}"))
                copy(pair_cols(bt, HI, p),
                     b_ps(f"TX{p}").rearrange("p (k n) -> p k n", k=KD)).then_inc(bt_hi, 1)

            def b_f(b, k):
                act.wait_ge(b_full, b_filled(b, f"F{k}"))
                if k // 2 >= 2:
                    act.wait_ge(stored[(k // 2) % 2], 48 * b + 16 * (k // 4))
                copy(f_part(k, HI), f_psum(k)).then_inc(f_hi, 1)

            def b_s(b, q):
                act.wait_ge(b_free[b_ring(f"S{q}")], b_read(b, f"S{q}"))
                act.activation(prob[:, q % 2, :], prob[:, q % 2, :], ACT.Exp, scale=ATT_SCALE)\
                    .then_inc(p_exp, 1)

            def b_pt(b, q):
                act.wait_ge(b_full, b_filled(b, f"PT{q}"))
                copy(pt_part(q, HI), b_ps(f"PT{q}")).then_inc(pt_hi, 1)

            def b_o(b, q):
                act.wait_ge(b_full, b_filled(b, f"O{q}"))
                for s in range(2):
                    act.wait_ge(stored[s], 48 * b + 48)
                copy(o_part(q, HI), o_psum(q)).then_inc(o_hi, 1)

            def b_tz(b, p):
                act.wait_ge(b_full, b_filled(b, f"TZ{p}"))
                copy(pair_cols(ct, HI, p),
                     b_ps(f"TZ{p}").rearrange("p (k n) -> p k n", k=KD)).then_inc(bt_hi, 1)

            def b_rout(b, h):
                act.wait_ge(b_full, b_filled(b, f"ROUT{h}"))
                copy(scores[:, 512 * h:512 * (h + 1)], b_ps(f"ROUT{h}")).then_inc(b_free[b_ring(f"ROUT{h}")], 1)

            def b_ff(b, p):
                act.wait_ge(ff_full, 4 * b + p + 1)
                act.wait_ge(ranked, b + 1)
                if p > 0:
                    act.wait_ge(gelu_used, 4 * b + p)
                act.activation(gelu[:, :, :].rearrange("p t n -> p (t n)"), m_bank[p][:, :],
                               ACT.Gelu_apprx_tanh, scale=1.0 / WS).then_inc(ff_read, 1)

            def normalise(dsts, srcs, k, side):
                for t in range(2):
                    ins = act.activation(dsts[t], srcs[t], ACT.Identity, bias=nm[side][:, k, t:t + 1],
                                         scale=rs[side][:, k, t:t + 1])
                return ins

            def a_apn(a, p):
                act.wait_ge(a_rs, 8 * a + p + 1)
                if later(a):
                    act.wait_ge(b_full, b_filled(a - 1, f"TX{p}"))
                    act.wait_ge(x3_copied, 4 * (a - 1) + p + 1)
                normalise([x1[:, 2 * p + t, :] for t in range(2)],
                          [a_ps(f"AP{p}")[:, D * t:D * (t + 1)] for t in range(2)], p, 0)\
                    .then_inc(a_free[a_ring(f"AP{p}")], 1)

            def a_moe(a, t):
                act.wait_ge(wt_ready, a + 1)
                for q in (2, 3):
                    act.wait_ge(m_full, 32 * a + 4 * t + q + 1)
                    if q == 2 and t >= 1:
                        act.wait_ge(moe_ready, T * a + t)
                    for h in range(2):
                        ins = copy(part[:, 2 * (q - 2) + h, :], m_bank[q][:, D * h:D * (h + 1)],
                                   wexp[:, t, 2 * q + h:2 * q + h + 1])
                    ins.then_inc(m_free[q], 1)
                act.wait_ge(m_free[3], T * a + t + 2)
                act.sem_inc(parted, 1)

            def a_ln2n(a, p):
                act.wait_ge(a_rs, 8 * a + 4 + p + 1)
                rows = [x2[:, 2 * p + t, :] for t in range(2)]
                normalise(rows, rows, 4 + p, 0).then_inc(x2_ready, 1)

            def b_prn(b, p):
                rows = [x3[:, 2 * p + t, :] for t in range(2)]
                act.wait_ge(b_rs, 8 * b + p + 1)
                normalise(rows, rows, p, 1).then_inc(x3_ready, 1)

            def b_res(b, p):
                act.wait_ge(ranked, b + 1)
                for t in range(2):
                    ins = copy(x3[:, 2 * p + t, :], x3[:, 2 * p + t, :], mres[:, 2 * p + t:2 * p + t + 1])
                ins.then_inc(x3_scaled, 1)

            def b_ffn(b, p):
                rows = [x3[:, 2 * p + t, :] for t in range(2)]
                act.wait_ge(b_rs, 8 * b + 4 + p + 1)
                normalise(rows, rows, 4 + p, 1).then_inc(y_ready, 1)

            def turn(a, b, c):
                if a is not None:
                    a_xs(a, 0)
                    a_xs(a, 1)
                if c is not None:
                    b_s(c, 0)
                    b_s(c, 1)
                if a is not None:
                    a_xs(a, 2)
                if b is not None:
                    a_moe(b, 0)
                if c is not None:
                    b_pt(c, 0)
                    b_s(c, 2)
                if a is not None:
                    a_xs(a, 3)
                if b is not None:
                    a_moe(b, 1)
                if c is not None:
                    b_pt(c, 1)
                    b_s(c, 3)
                if a is not None:
                    a_gram(a, 0)
                if c is not None:
                    b_pt(c, 2)
                if a is not None:
                    a_gram(a, 1)
                if c is not None:
                    b_pt(c, 3)
                    b_o(c, 0)
                    b_o(c, 1)
                    b_o(c, 2)
                    b_o(c, 3)
                if b is not None:
                    a_moe(b, 2)
                if a is not None:
                    a_srow(a)
                if b is not None:
                    a_ln2n(b, 0)
                    a_moe(b, 3)
                if c is not None:
                    b_prn(c, 0)
                    b_prn(c, 1)
                    b_tz(c, 0)
                    b_prn(c, 2)
                if a is not None:
                    to_at_hi(a, "TX0", 0, 0)
                if c is not None:
                    b_tz(c, 1)
                    b_prn(c, 3)
                if a is not None:
                    a_t(a, 0)
                if c is not None:
                    b_tz(c, 2)
                    b_tz(c, 3)
                if a is not None:
                    a_t(a, 1)
                if c is not None:
                    b_rout(c, 0)
                    b_rout(c, 1)
                if a is not None:
                    a_trow(a)
                    to_at_hi(a, "TX1", 1, 1)
                if b is not None:
                    a_moe(b, 4)
                    a_ln2n(b, 1)
                    a_moe(b, 5)
                    a_moe(b, 6)
                if a is not None:
                    a_iq(a)
                if b is not None:
                    a_ln2n(b, 2)
                    b_tx(b, 0)
                if a is not None:
                    a_m(a)
                    to_at_hi(a, "TX2", 2, 2)
                if c is not None:
                    b_res(c, 0)
                if b is not None:
                    a_moe(b, 7)
                if a is not None:
                    a_cb(a)
                if c is not None:
                    b_ff(c, 0)
                    b_res(c, 1)
                    b_ff(c, 1)
                    b_res(c, 2)
                    b_res(c, 3)
                if a is not None:
                    to_at_hi(a, "TX3", 3, 3)
                if b is not None:
                    b_tx(b, 1)
                if c is not None:
                    b_ffn(c, 0)
                if b is not None:
                    b_tx(b, 2)
                    a_ln2n(b, 3)
                if c is not None:
                    b_ffn(c, 1)
                if b is not None:
                    b_tx(b, 3)
                if c is not None:
                    b_ff(c, 2)
                if b is not None:
                    b_f(b, 0)
                    b_f(b, 1)
                if c is not None:
                    b_ff(c, 3)
                if a is not None:
                    a_apn(a, 0)
                if b is not None:
                    b_f(b, 2)
                if c is not None:
                    b_ffn(c, 2)
                if b is not None:
                    b_f(b, 3)
                if a is not None:
                    to_at_hi(a, "TY0", 0, 4)
                    a_apn(a, 1)
                if b is not None:
                    b_f(b, 4)
                if c is not None:
                    b_ffn(c, 3)
                if b is not None:
                    b_f(b, 5)
                if a is not None:
                    to_at_hi(a, "TY1", 1, 5)
                if b is not None:
                    b_f(b, 6)
                if a is not None:
                    a_apn(a, 2)
                if b is not None:
                    b_f(b, 7)
                    b_f(b, 8)
                if a is not None:
                    to_at_hi(a, "TY2", 2, 6)
                    a_apn(a, 3)
                if b is not None:
                    b_f(b, 9)
                if a is not None:
                    to_at_hi(a, "TY3", 3, 7)
                if b is not None:
                    b_f(b, 10)
                if a is not None:
                    a_gate(a)
                if b is not None:
                    b_f(b, 11)
                if a is not None:
                    a_wt(a)

            turn(0, None, None)
            turn(1, 0, None)
            with act.Fori(2, NB) as i:
                turn(i, i - 1, i - 2)
            turn(None, NB - 1, NB - 2)
            turn(None, None, NB - 1)

        @block.vector
        def _(dve):
            def split_lo(dst, src, hi):
                return dve.tensor_tensor(dst, src, hi, ALU.subtract)

            dve.wait_ge(w_loaded, 16 * N_LOADS)
            for n, (w, src, scale) in enumerate(SPLITS):
                dve.wait_ge(w_hi, n + 1)
                dve.scalar_tensor_tensor(out=w[:, LO, :, :], in0=src, scalar=scale, in1=w[:, HI, :, :],
                                         op0=ALU.mult, op1=ALU.subtract).then_inc(w_lo, 1)
            dve.wait_ge(w_hi, N_SPLITS + 1)
            split_lo(bproj16[32:33, :], rowin[32:33, 0:D], rowtmp[32:33, 0:D])
            dve.scalar_tensor_tensor(out=gb16[32:33, :], in0=rowin[32:33, D:D + E], scalar=WS,
                                     in1=rowtmp[32:33, D:D + E], op0=ALU.mult, op1=ALU.subtract)\
                .then_inc(w_lo, 1)

            done_a = StepCount(A_STEPS)
            done_b = StepCount(B_STEPS)

            def transposed_lo(dst, ps, hi):
                return split_lo(dst, ps.rearrange("p (k n) -> p k n", k=KD), hi)

            def pair_stats(srcs, n, k, side):
                if k > 0 or side == 0 and later(n):
                    dve.wait_ge((a_mv, b_mv)[side], 8 * n + k)
                for t in range(2):
                    ins = dve.bn_stats(stats[side][:, t, :], srcs[t])
                ins.then_inc(bn_done[side], 1)
                dve.wait_ge(bn_done[side], 8 * n + k + 1)
                dve.sem_inc(waits_held, 1)
                for t in range(2):
                    ins = dve.bn_aggr(mv[side][:, k, t, :], stats[side][:, t, :])
                ins.then_inc((a_mv, b_mv)[side], 1)

            def to_at_lo(a, name, p, n):
                dve.wait_ge(at_hi, 8 * a + n + 1)
                transposed_lo(pair_cols(at, LO, p), a_ps(name), pair_cols(at, HI, p)).then_inc(a_free[a_ring(name)], 1)

            def a_tx(a, p):
                to_at_lo(a, f"TX{p}", p, p)

            def a_t(a, m):
                dve.wait_ge(t_copied, 3 * a + m + 1)
                dve.tensor_tensor(prod[:, m, :], a_ps(f"T{m}"), wqk[:, m, :], ALU.mult).then_inc(a_free[a_ring(f"T{m}")], 1)

            def a_trow(a):
                dve.wait_ge(t_copied, 3 * a + 3)
                dve.tensor_tensor(prow[:, :], a_ps("TROW")[0:1, :], brow[:, :], ALU.mult).then_inc(a_free[a_ring("TROW")], 1)

            def a_norm(a):
                dve.wait_ge(a_full, a_filled(a, "NORM"))
                dve.tensor_copy(nrm[:, :], a_ps("NORM")[:, 0:4]).then_inc(a_free[a_ring("NORM")], 1)

            def a_g(a):
                dve.wait_ge(a_full, a_filled(a, "G"))
                dve.wait_ge(inv_ready, a + 1)
                for t in range(2):
                    ins = dve.tensor_scalar(diag[:, t, :], ident, inv[:, t:t + 1], None, ALU.mult)
                ins.then_inc(diag_ready, 1)
                for m in range(KD):
                    ins = dve.tensor_scalar(gsc[:, m, :], a_ps("G")[:, D * m:D * (m + 1)],
                                            inv[:, 2 + m:3 + m], None, ALU.mult)
                ins.then_inc(a_free[a_ring("G")], 1)

            def a_csum(a):
                dve.wait_ge(a_free[a_ring("IQ")], a_read(a, "IQ"))
                dve.wait_ge(a_free[a_ring("G")], a_read(a, "G"))
                dve.tensor_tensor(g1, gsc, iq[:, None, :].broadcast_to([P, KD, D]), ALU.mult).then_inc(v_step_a, 1)
                dve.wait_ge(v_step_a, done_a.next(a))
                dve.tensor_scalar(g1, g1, 1.0, None, ALU.add).then_inc(g1_ready, 1)
                dve.wait_ge(a_full, a_filled(a, "CSUM"))
                dve.tensor_tensor(den, a_ps("CSUM")[:, 0:D], iq[:, :], ALU.mult).then_inc(a_free[a_ring("CSUM")], 1)
                dve.wait_ge(a_free[a_ring("CSUM")], a_read(a, "CSUM"))
                dve.tensor_scalar(den, den, float(D), None, ALU.add).then_inc(v_step_a, 1)
                dve.wait_ge(v_step_a, done_a.next(a))
                dve.reciprocal(gt[:, :], den).then_inc(v_step_a, 1)
                dve.wait_ge(v_step_a, done_a.next(a))
                dve.tensor_scalar(gt[:, :], gt[:, :], gam[:, 0:1], None, ALU.mult).then_inc(v_step_a, 1)
                dve.wait_ge(v_step_a, done_a.next(a))

            def a_m(a):
                dve.wait_ge(a_full, a_filled(a, "M"))
                m3 = m32.rearrange("p (k n) -> p k n", k=KD)
                dve.tensor_tensor(m3, a_ps("M").rearrange("p (k n) -> p k n", k=KD),
                                          gt[:, None, :].broadcast_to([P, KD, D]), ALU.mult).then_inc(a_free[a_ring("M")], 1)
                dve.wait_ge(a_free[a_ring("M")], a_read(a, "M"))
                for k in range(KD):
                    d = m3[:, k, P * k:P * (k + 1)]
                    ins = dve.scalar_tensor_tensor(out=d, in0=ident, scalar=2.0, in1=d, op0=ALU.mult,
                                                   op1=ALU.add)
                ins.then_inc(m32_ready, 1)
                dve.wait_ge(m_hi, a + 1)
                split_lo(m16[:, LO, :, :].rearrange("p k n -> p (k n)"), m32,
                         m16[:, HI, :, :].rearrange("p k n -> p (k n)")).then_inc(m_lo, 1)

            def a_cb(a):
                dve.wait_ge(a_full, a_filled(a, "CB"))
                dve.tensor_tensor(c32[:, :], a_ps("CB")[:, 0:D], gt[:, :], ALU.mult).then_inc(a_free[a_ring("CB")], 1)
                dve.wait_ge(c_hi, a + 1)
                split_lo(c16[32:33, :], c32[32:33, :], rowtmp[32:33, 0:D]).then_inc(c_lo, 1)

            def a_ap(a, p):
                dve.wait_ge(a_full, a_filled(a, f"AP{p}"))
                src = [a_ps(f"AP{p}")[:, D * t:D * (t + 1)] for t in range(2)]
                pair_stats(src, a, p, 0)

            def a_gate(a):
                dve.wait_ge(a_full, a_filled(a, "GATE"))
                ps = a_ps("GATE")[:, 0:T * E].rearrange("p (t e) -> p t e", e=E)
                bc = lambda v: v[:, :, None].broadcast_to([P, T, E])
                dve.tensor_reduce(gs[:, :], ps, X, ALU.max).then_inc(v_step_a, 1)
                dve.wait_ge(v_step_a, done_a.next(a))
                dve.tensor_tensor(gl[:, :, :], ps, bc(gs), ALU.subtract).then_inc(a_free[a_ring("GATE")], 1)
                dve.wait_ge(gexp, a + 1)
                dve.tensor_reduce(gs[:, :], ge[:, :, :], X, ALU.add).then_inc(v_step_a, 1)
                dve.wait_ge(v_step_a, done_a.next(a))
                dve.reciprocal(gr[:, :], gs[:, :]).then_inc(v_step_a, 1)
                dve.wait_ge(v_step_a, done_a.next(a))
                dve.tensor_tensor(ge[:, :, :], ge[:, :, :], bc(gr), ALU.mult).then_inc(v_step_a, 1)
                dve.wait_ge(v_step_a, done_a.next(a))
                dve.scalar_tensor_tensor(out=gl[:, :, :], in0=ge[:, :, :], scalar=THRESHOLD,
                                              in1=ge[:, :, :], op0=ALU.is_ge, op1=ALU.mult).then_inc(v_step_a, 1)
                dve.wait_ge(v_step_a, done_a.next(a))
                dve.tensor_reduce(gs[:, :], gl[:, :, :], X, ALU.add).then_inc(v_step_a, 1)
                dve.wait_ge(v_step_a, done_a.next(a))
                dve.scalar_tensor_tensor(out=gr[:, :], in0=gs[:, :], scalar=0.0, in1=gs[:, :],
                                              op0=ALU.is_equal, op1=ALU.add).then_inc(v_step_a, 1)
                dve.wait_ge(v_step_a, done_a.next(a))
                dve.reciprocal(gs[:, :], gr[:, :]).then_inc(v_step_a, 1)
                dve.wait_ge(v_step_a, done_a.next(a))
                dve.tensor_tensor(w32[:, :, :], gl[:, :, :], bc(gs), ALU.mult).then_inc(v_step_a, 1)
                dve.wait_ge(v_step_a, done_a.next(a))
                dve.tensor_scalar(wexp[:, :, :], w32[:, :, :], 1.0 / WS, None, ALU.mult)\
                    .then_inc(wt_ready, 1)

            def a_wt(a):
                dve.wait_ge(wt_hi, a + 1)
                split_lo(w16t[0:T * E, LO, :], a_ps("WT")[0:T * E, 0:P], w16t[0:T * E, HI, :]).then_inc(a_free[a_ring("WT")], 1)

            def a_bias(a, p):
                dve.wait_ge(a_full, a_filled(a, f"BIAS{p}"))
                pair = x1[:, 2 * p:2 * p + 2, :]
                dve.tensor_tensor(pair, a_ps(f"BIAS{p}").rearrange("p (t n) -> p t n", t=2), pair, ALU.add)\
                    .then_inc(a_free[a_ring(f"BIAS{p}")], 1)

            def a_moe(a, t):
                dst = x1[:, t, :]
                if t % 2 == 0:
                    dve.wait_ge(a_free[a_ring(f"BIAS{t // 2}")], a_read(a, f"BIAS{t // 2}"))
                for e in range(4):
                    q = e // 2
                    if e % 2 == 0:
                        dve.wait_ge(m_full, 32 * a + 4 * t + q + 1)
                    ins = dve.scalar_tensor_tensor(out=dst, in0=m_bank[q][:, D * (e % 2):D * (e % 2 + 1)],
                                                   scalar=wexp[:, t, e:e + 1], in1=dst, op0=ALU.mult,
                                                   op1=ALU.add)
                    if e % 2 == 0:
                        ins.then_inc(m_step, 1)
                        dve.wait_ge(m_step, 2 * T * a + 2 * t + q + 1)
                    else:
                        ins.then_inc(m_free[q], 1)
                        if q == 0:
                            dve.wait_ge(m_free[q], T * a + t + 2)
                dve.wait_ge(m_free[1], T * a + t + 2)
                dve.sem_inc(chained, 1)

            def a_ln2(a, p):
                dve.wait_ge(moe_ready, T * a + 2 * p + 2)
                pair_stats([x1[:, 2 * p + t, :] for t in range(2)], a, 4 + p, 0)

            def b_tx(b, p):
                dve.wait_ge(bt_hi, 8 * b + p + 1)
                transposed_lo(pair_cols(bt, LO, p), b_ps(f"TX{p}"), pair_cols(bt, HI, p)).then_inc(b_free[b_ring(f"TX{p}")], 1)

            def b_f(b, k):
                dve.wait_ge(f_hi, 12 * b + k + 1)
                split_lo(f_part(k, LO), f_psum(k), f_part(k, HI)).then_inc(b_free[b_ring(f"F{k}")], 1)

            def b_s(b, q):
                dve.wait_ge(b_full, b_filled(b, f"S{q}"))
                ps = b_ps(f"S{q}").rearrange("p (a g) -> p a g", g=H)
                pr = prob[:, q % 2, :].rearrange("p (a g) -> p a g", g=H)
                dve.tensor_reduce(smax[:, :], ps, X, ALU.max).then_inc(v_step_b, 1)
                dve.wait_ge(v_step_b, done_b.next(b))
                dve.tensor_tensor(pr, ps, smax[:, :, None].broadcast_to([P, 32, H]),
                                          ALU.subtract).then_inc(b_free[b_ring(f"S{q}")], 1)
                dve.wait_ge(p_exp, 4 * b + q + 1)
                dve.tensor_reduce(ssum[:, :], pr, X, ALU.add).then_inc(v_step_b, 1)
                dve.wait_ge(v_step_b, done_b.next(b))
                dve.reciprocal(srec[:, q % 2, :], ssum[:, :]).then_inc(p_rec, 1)

            def b_pt(b, q):
                dve.wait_ge(pt_hi, 4 * b + q + 1)
                split_lo(pt_part(q, LO), b_ps(f"PT{q}"), pt_part(q, HI)).then_inc(b_free[b_ring(f"PT{q}")], 1)

            def b_o(b, q):
                dve.wait_ge(o_hi, 4 * b + q + 1)
                split_lo(o_part(q, LO), o_psum(q), o_part(q, HI)).then_inc(b_free[b_ring(f"O{q}")], 1)

            def b_pr(b, p):
                dve.wait_ge(b_full, b_filled(b, f"PR{p}"))
                dve.wait_ge(x3_copied, 4 * b + p + 1)
                pair = x3[:, 2 * p:2 * p + 2, :]
                dve.tensor_tensor(pair, b_ps(f"PR{p}").rearrange("p (t n) -> p t n", t=2),
                                          pair, ALU.add).then_inc(b_free[b_ring(f"PR{p}")], 1)
                dve.wait_ge(b_free[b_ring(f"PR{p}")], b_read(b, f"PR{p}"))
                pair_stats([x3[:, 2 * p + t, :] for t in range(2)], b, p, 1)

            def b_tz(b, p):
                dve.wait_ge(bt_hi, 8 * b + 4 + p + 1)
                transposed_lo(pair_cols(ct, LO, p), b_ps(f"TZ{p}"), pair_cols(ct, HI, p)).then_inc(b_free[b_ring(f"TZ{p}")], 1)

            def b_scol(b, h):
                dve.wait_ge(b_full, b_filled(b, f"SCOL{h}"))
                dve.tensor_copy(scol[:, 4 * h:4 * h + 4], b_ps(f"SCOL{h}")[:, 0:4]).then_inc(b_free[b_ring(f"SCOL{h}")], 1)

            def b_rank(b, t):
                if t == 0:
                    dve.wait_ge(b_free[b_ring("SCOL0")], b_read(b, "SCOL0"))
                    dve.wait_ge(b_free[b_ring("SCOL1")], b_read(b, "SCOL1"))
                    dve.sem_inc(waits_held, 1)
                    dve.wait_ge(b_free[b_ring("ROUT1")], b_read(b, "ROUT1"))
                    dve.memset(rank3[:, 0, 1:2], 0.0)
                me = scol[:, t:t + 1]
                if t > 0:
                    dve.tensor_scalar(rjunk[:, 0:P * t], scores[:, 0:P * t], me, None, ALU.is_ge,
                                      ALU.add, accum_out=rank3[:, t, 1:2])
                dve.tensor_scalar(rjunk[:, P * t:C], scores[:, P * t:C], me, None, ALU.is_gt,
                                  ALU.add, accum_out=rank3[:, t, 0:1])
                dve.scalar_tensor_tensor(out=rjunk2[:, :], in0=scores[:, P * t:P * (t + 1)],
                                         scalar=me, in1=lower, op0=ALU.is_equal, op1=ALU.mult,
                                         accum_out=rank3[:, t, 2:3]).then_inc(v_step_b, 1)
                dve.wait_ge(v_step_b, done_b.next(b))

            def b_select(b):
                dve.tensor_reduce(rank[:, :], rank3[:, :, :], X, ALU.add).then_inc(v_step_b, 1)
                dve.wait_ge(v_step_b, done_b.next(b))
                dve.tensor_scalar(msel[:, :], rank[:, :], float(KEEP), None, ALU.is_lt).then_inc(v_step_b, 1)
                dve.wait_ge(v_step_b, done_b.next(b))
                dve.tensor_scalar(mres[:, :], msel[:, :], -1.0, 2.0, ALU.mult, ALU.add).then_inc(ranked, 1)

            def b_ff(b, p):
                rows = [x3[:, 2 * p + t, :] for t in range(2)]
                dve.wait_ge(x3_scaled, 4 * b + p + 1)
                dve.wait_ge(ff_read, 4 * (b + 1) + p + 1)
                for t in range(2):
                    ins = dve.scalar_tensor_tensor(out=rows[t], in0=gelu[:, t, :],
                                                   scalar=msel[:, 2 * p + t:2 * p + t + 1], in1=rows[t],
                                                   op0=ALU.mult, op1=ALU.add)
                ins.then_inc(gelu_used, 1)
                dve.wait_ge(gelu_used, 4 * b + p + 1)
                pair_stats(rows, b, 4 + p, 1)

            def turn(a, b, c):
                if c is not None:
                    b_s(c, 0)
                    b_s(c, 1)
                if b is not None:
                    a_moe(b, 0)
                if c is not None:
                    b_pt(c, 0)
                    b_s(c, 2)
                if b is not None:
                    a_moe(b, 1)
                if c is not None:
                    b_pt(c, 1)
                    b_s(c, 3)
                    b_pt(c, 2)
                    b_pt(c, 3)
                    b_o(c, 0)
                    b_o(c, 1)
                    b_o(c, 2)
                if b is not None:
                    a_ln2(b, 0)
                if c is not None:
                    b_o(c, 3)
                if b is not None:
                    a_moe(b, 2)
                    a_moe(b, 3)
                if c is not None:
                    b_pr(c, 0)
                    b_pr(c, 1)
                    b_pr(c, 2)
                    b_pr(c, 3)
                    b_tz(c, 0)
                if a is not None:
                    a_tx(a, 0)
                if c is not None:
                    b_tz(c, 1)
                if a is not None:
                    a_t(a, 0)
                if c is not None:
                    b_tz(c, 2)
                    b_tz(c, 3)
                if a is not None:
                    a_t(a, 1)
                if b is not None:
                    a_ln2(b, 1)
                if c is not None:
                    b_scol(c, 0)
                if a is not None:
                    a_trow(a)
                    a_tx(a, 1)
                if c is not None:
                    b_scol(c, 1)
                    b_rank(c, 0)
                if b is not None:
                    a_moe(b, 4)
                if c is not None:
                    b_rank(c, 1)
                    b_rank(c, 2)
                    b_rank(c, 3)
                if a is not None:
                    a_norm(a)
                if c is not None:
                    b_rank(c, 4)
                if b is not None:
                    a_moe(b, 5)
                if c is not None:
                    b_rank(c, 5)
                    b_rank(c, 6)
                if a is not None:
                    a_g(a)
                if b is not None:
                    a_ln2(b, 2)
                    a_moe(b, 6)
                if c is not None:
                    b_rank(c, 7)
                    b_select(c)
                if a is not None:
                    a_csum(a)
                if b is not None:
                    b_tx(b, 0)
                if a is not None:
                    a_m(a)
                    a_tx(a, 2)
                if b is not None:
                    a_moe(b, 7)
                if a is not None:
                    a_cb(a)
                if c is not None:
                    b_ff(c, 0)
                if b is not None:
                    a_ln2(b, 3)
                if c is not None:
                    b_ff(c, 1)
                if a is not None:
                    a_tx(a, 3)
                if b is not None:
                    b_tx(b, 1)
                if a is not None:
                    a_ap(a, 0)
                if b is not None:
                    b_tx(b, 2)
                if a is not None:
                    a_ap(a, 1)
                if b is not None:
                    b_tx(b, 3)
                if c is not None:
                    b_ff(c, 2)
                if b is not None:
                    b_f(b, 0)
                    b_f(b, 1)
                if c is not None:
                    b_ff(c, 3)
                if b is not None:
                    b_f(b, 2)
                    b_f(b, 3)
                if a is not None:
                    to_at_lo(a, "TY0", 0, 4)
                if b is not None:
                    b_f(b, 4)
                    b_f(b, 5)
                if a is not None:
                    to_at_lo(a, "TY1", 1, 5)
                    a_ap(a, 2)
                if b is not None:
                    b_f(b, 6)
                if a is not None:
                    a_ap(a, 3)
                if b is not None:
                    b_f(b, 7)
                    b_f(b, 8)
                if a is not None:
                    to_at_lo(a, "TY2", 2, 6)
                if b is not None:
                    b_f(b, 9)
                if a is not None:
                    to_at_lo(a, "TY3", 3, 7)
                if b is not None:
                    b_f(b, 10)
                if a is not None:
                    a_gate(a)
                if b is not None:
                    b_f(b, 11)
                if a is not None:
                    a_wt(a)
                    a_bias(a, 0)
                    a_bias(a, 1)
                    a_bias(a, 2)
                    a_bias(a, 3)

            turn(0, None, None)
            turn(1, 0, None)
            with dve.Fori(2, NB) as i:
                turn(i, i - 1, i - 2)
            turn(None, NB - 1, NB - 2)
            turn(None, None, NB - 1)
            assert done_a.done % A_STEPS == 0 and done_b.done % B_STEPS == 0

        @block.tensor
        def _(pe):
            def sum_of(dst, terms):
                for n, (lhs, rhs) in enumerate(terms):
                    ins = pe.matmul(dst, lhs, rhs, start=(n == 0), stop=(n == len(terms) - 1))
                return ins

            def split_terms(lhs, rhs):
                return [(lhs(k, i), rhs(k, j)) for k in range(KD) for i, j in PASSES]

            def transpose_pair(ps, src, p):
                for k in range(KD):
                    for t in range(2):
                        ins = pe.transpose(ps[:, 2 * P * k + P * t:2 * P * k + P * (t + 1)],
                                           src[:, 2 * p + t, P * k:P * (k + 1)], ident)
                return ins

            def tok(t):
                return slice(P * t, P * (t + 1))

            pe.wait_ge(init_p, 3)
            pe.wait_ge(w_hi, N_SPLITS + 1)
            pe.wait_ge(w_lo, N_SPLITS + 1)

            def a_tx(a, p):
                pe.wait_ge(x_ready[p], 16 * (a + 1))
                pe.wait_ge(a_free[a_ring(f"TX{p}")], a_before(a, f"TX{p}"))
                transpose_pair(a_ps(f"TX{p}"), x_in, p).then_inc(a_full, 1)

            def a_gram(a, m):
                pe.wait_ge(xs_lo, 4 * (a + 1))
                pe.wait_ge(a_free[a_ring(f"GRAM{m}")], a_before(a, f"GRAM{m}"))
                cols = slice(P * m, P * (m + 1))
                sum_of(a_ps(f"GRAM{m}")[:, 0:D],
                       [(xs[:, t, i, cols], xs[:, t, j, :]) for t in range(T) for i, j in PASSES])
                sum_of(a_ps(f"GRAM{m}")[:, D:D + 1],
                       [(xs[:, t, i, cols], ones16[:, :]) for t in range(T) for i in (HI, LO)])\
                    .then_inc(a_full, 1)

            def a_srow(a):
                pe.wait_ge(a_free[a_ring("SROW")], a_before(a, "SROW"))
                pe.wait_ge(a_free[1 - a_ring("SROW")], a_other(a, "SROW", ("GRAM0", "GRAM1")))
                for m in range(KD):
                    ins = pe.transpose(a_ps("SROW")[0:1, P * m:P * (m + 1)], gram[:, m, D:D + 1], ident)
                ins.then_inc(a_full, 1)

            def a_t(a, m):
                pe.wait_ge(a_free[a_ring(f"T{m}")], a_before(a, f"T{m}"))
                pe.wait_ge(a_free[1 - a_ring(f"T{m}")], a_other(a, f"T{m}", ("SROW",)))
                sum_of(a_ps(f"T{m}"), [(gram[:, k, P * m:P * (m + 1)], wqk[:, k, :]) for k in range(KD)]
                       + [(srow[0:1, P * m:P * (m + 1)], brow[0:1, :])]).then_inc(a_full, 1)

            def a_trow(a):
                pe.wait_ge(a_free[a_ring("TROW")], a_before(a, "TROW"))
                sum_of(a_ps("TROW")[0:1, :], [(gram[:, k, D:D + 1], wqk[:, k, :]) for k in range(KD)]
                       + [(c_one[0:1, 0:1], brow[0:1, :])]).then_inc(a_full, 1)

            def a_norm(a):
                pe.wait_ge(a_free[a_ring("NORM")], a_before(a, "NORM"))
                pe.wait_ge(a_free[1 - a_ring("NORM")], a_other(a, "NORM", ("T0", "T1", "TROW")))
                for c in range(4):
                    ins = sum_of(a_ps("NORM")[:, c:c + 1],
                                 [(prod[:, k, P * c:P * (c + 1)], ones[:, 0:1]) for k in range(KD)]
                                 + [(prow[0:1, P * c:P * (c + 1)], ones[0:1, 0:1])])
                ins.then_inc(a_full, 1)

            def a_g(a):
                pe.wait_ge(t_copied, 3 * a + 3)
                pe.wait_ge(a_free[a_ring("G")], a_before(a, "G"))
                for m in range(KD):
                    cols = slice(D + P * m, D + P * (m + 1))
                    ins = sum_of(a_ps("G")[:, D * m:D * (m + 1)],
                                 [(wqk[:, k, cols], tq[:, k, :]) for k in range(KD)]
                                 + [(brow[0:1, cols], trow[0:1, 0:D])])
                ins.then_inc(a_full, 1)

            def a_iq(a):
                pe.wait_ge(diag_ready, a + 1)
                pe.wait_ge(a_free[a_ring("IQ")], a_before(a, "IQ"))
                pe.matmul(a_ps("IQ")[:, 0:D], ones[:, :], diag.rearrange("p k n -> p (k n)"),
                          start=True, stop=True).then_inc(a_full, 1)

            def a_csum(a):
                pe.wait_ge(a_free[a_ring("CSUM")], a_before(a, "CSUM"))
                pe.wait_ge(a_free[1 - a_ring("CSUM")], a_other(a, "CSUM", ("G",)))
                sum_of(a_ps("CSUM")[:, 0:D], [(ones[:, :], gsc[:, k, :]) for k in range(KD)]
                       + [(eps_row[0:1, :], trow[0:1, 0:D])]).then_inc(a_full, 1)

            def a_m(a):
                pe.wait_ge(g1_ready, a + 1)
                pe.wait_ge(a_free[a_ring("M")], a_before(a, "M"))
                for m in range(KD):
                    ins = sum_of(a_ps("M")[:, D * m:D * (m + 1)],
                                 [(wvs[:, k, P * m:P * (m + 1)], g1[:, k, :]) for k in range(KD)])
                ins.then_inc(a_full, 1)

            def a_cb(a):
                pe.wait_ge(a_free[a_ring("CB")], a_before(a, "CB"))
                sum_of(a_ps("CB")[:, 0:D], [(bvr[:, k, :], g1[:, k, :]) for k in range(KD)])\
                    .then_inc(a_full, 1)

            def a_ap(a, p):
                pe.wait_ge(m_lo, a + 1)
                pe.wait_ge(c_lo, a + 1)
                pe.wait_ge(a_free[a_ring(f"AP{p}")], a_before(a, f"AP{p}"))
                for t in range(2):
                    ins = sum_of(a_ps(f"AP{p}")[:, D * t:D * (t + 1)],
                                 split_terms(lambda k, i: at[:, k, i, tok(2 * p + t)],
                                             lambda k, j: m16[:, j, k, :]) + [(rows16[:, :], c16[:, :])])
                ins.then_inc(a_full, 1)

            def a_ty(a, p):
                pe.wait_ge(a_free[a_ring(f"TY{p}")], a_before(a, f"TY{p}"))
                pe.wait_ge(a_free[1 - a_ring(f"TY{p}")], a_other(a, f"TY{p}", (f"AP{p}",)))
                transpose_pair(a_ps(f"TY{p}"), x1, p).then_inc(a_full, 1)

            def a_gate(a):
                pe.wait_ge(a_free[a_ring("GATE")], a_before(a, "GATE"))
                pe.wait_ge(a_free[1 - a_ring("GATE")], a_other(a, "GATE", [f"TY{p}" for p in range(TP)]))
                for t in range(T):
                    ins = sum_of(a_ps("GATE")[:, E * t:E * (t + 1)],
                                 split_terms(lambda k, i: at[:, k, i, tok(t)],
                                             lambda k, j: gw[:, j, k, :]) + [(rows16[:, :], gb16[:, :])])
                ins.then_inc(a_full, 1)

            def a_wt(a):
                pe.wait_ge(wt_ready, a + 1)
                pe.wait_ge(a_free[a_ring("WT")], a_before(a, "WT"))
                pe.sem_inc(waits_held, 1)
                pe.transpose(a_ps("WT")[0:T * E, 0:P], w32[:, :, :].rearrange("p t e -> p (t e)"), ident)\
                    .then_inc(a_full, 1)

            def a_bias(a, p):
                pe.wait_ge(a_free[a_ring(f"BIAS{p}")], a_before(a, f"BIAS{p}"))
                pe.wait_ge(a_free[1 - a_ring(f"BIAS{p}")], a_other(a, f"BIAS{p}", ("WT",)))
                for t in range(2):
                    ins = sum_of(a_ps(f"BIAS{p}")[:, D * t:D * (t + 1)],
                                 [(w16t[:, i, :], ebd[:, j, 2 * p + t, :]) for i, j in PASSES])
                ins.then_inc(a_full, 1)

            def a_moe(a, t):
                for q in range(4):
                    if t == 0 and later(a):
                        pe.wait_ge(ff_read, 4 * (a - 1) + q + 1)
                    pe.wait_ge(m_free[q], T * a + t + 1)
                    sum_of(m_bank[q][:, :], split_terms(lambda k, i: at[:, k, i, tok(t)],
                                                        lambda k, j: we[:, j, k, 512 * q:512 * (q + 1)]))\
                        .then_inc(m_full, 1)

            def b_tx(b, p):
                pe.wait_ge(x2_ready, 4 * b + p + 1)
                pe.wait_ge(b_free[b_ring(f"TX{p}")], b_before(b, f"TX{p}"))
                transpose_pair(b_ps(f"TX{p}"), x2, p).then_inc(b_full, 1)

            def b_f(b, k):
                ft, hf = k // 2, k % 2
                pe.wait_ge(b_free[b_ring(f"F{k}")], b_before(b, f"F{k}"))
                pe.wait_ge(b_free[1 - b_ring(f"F{k}")], b_other(b, f"F{k}", (f"TX{2 * hf}", f"TX{2 * hf + 1}")))
                sum_of(b_ps(f"F{k}"), split_terms(lambda k, i: wqkv[:, i, k, P * ft:P * (ft + 1)],
                                                  lambda k, j: bt[:, k, j, 512 * hf:512 * (hf + 1)]))\
                    .then_inc(b_full, 1)

            def b_s(b, q):
                pe.wait_ge(qk_loaded, 32 * T * (b + 1))
                pe.wait_ge(b_free[b_ring(f"S{q}")], b_before(b, f"S{q}"))
                for c in range(4):
                    for g in range(T):
                        token = 16 * g + 4 * q + c
                        n = T * c + g
                        ins = sum_of(b_ps(f"S{q}")[:, H * n:H * (n + 1)],
                                     [(blockdiag[:, :, P * i + token], keys[:, :, P * j + token])
                                      for i, j in PASSES])
                ins.then_inc(b_full, 1)

            def b_pt(b, q):
                pe.wait_ge(p_ready, 4 * b + q + 1)
                pe.wait_ge(b_free[b_ring(f"PT{q}")], b_before(b, f"PT{q}"))
                for c in range(4):
                    ins = pe.transpose(b_ps(f"PT{q}")[:, P * c:P * (c + 1)],
                                       prob[:, q % 2, P * c:P * (c + 1)], ident)
                ins.then_inc(b_full, 1)

            def b_o(b, q):
                pe.wait_ge(v_loaded, 16 * T * (b + 1))
                pe.wait_ge(b_free[b_ring(f"O{q}")], b_before(b, f"O{q}"))
                pe.wait_ge(b_free[1 - b_ring(f"O{q}")], b_other(b, f"O{q}", (f"PT{q}",)))
                for c in range(4):
                    for r in range(T):
                        token = 16 * r + 4 * q + c
                        n = T * c + r
                        ins = sum_of(b_ps(f"O{q}")[:, H * n:H * (n + 1)],
                                     [(blockdiag[:, :, P * i + token],
                                       probs_t[:, j, 4 * q + c, H * r:H * (r + 1)]) for i, j in PASSES])
                ins.then_inc(b_full, 1)

            def b_pr(b, p):
                pe.wait_ge(o_loaded, 16 * KD * (b + 1))
                pe.wait_ge(b_free[b_ring(f"PR{p}")], b_before(b, f"PR{p}"))
                heads = [bt[:, k, :, :].rearrange("p l n -> p (l n)")
                         .rearrange("p (b l n) -> p b l n", b=T, l=2) for k in range(KD)]
                for t in range(2):
                    ins = sum_of(b_ps(f"PR{p}")[:, D * t:D * (t + 1)],
                                 split_terms(lambda k, i: heads[k][:, 2 * p + t, i, :],
                                             lambda k, j: wproj[:, j, k, :])
                                 + [(rows16[:, :], bproj16[:, :])])
                ins.then_inc(b_full, 1)

            def b_tz(b, p):
                pe.wait_ge(x3_ready, 4 * b + p + 1)
                pe.wait_ge(b_free[b_ring(f"TZ{p}")], b_before(b, f"TZ{p}"))
                transpose_pair(b_ps(f"TZ{p}"), x3, p).then_inc(b_full, 1)

            def b_rout(b, h):
                pe.wait_ge(b_free[b_ring(f"ROUT{h}")], b_before(b, f"ROUT{h}"))
                pe.wait_ge(b_free[1 - b_ring(f"ROUT{h}")], b_other(b, f"ROUT{h}", (f"TZ{2 * h}", f"TZ{2 * h + 1}")))
                sum_of(b_ps(f"ROUT{h}"), split_terms(lambda k, i: wrt[:, i, k, :],
                                                     lambda k, j: ct[:, k, j, 512 * h:512 * (h + 1)]))\
                    .then_inc(b_full, 1)

            def b_scol(b, h):
                pe.wait_ge(b_free[b_ring(f"SCOL{h}")], b_before(b, f"SCOL{h}"))
                pe.wait_ge(b_free[1 - b_ring(f"SCOL{h}")], b_other(b, f"SCOL{h}", (f"ROUT{h}",)))
                pe.sem_inc(waits_held, 1)
                for t in range(4):
                    ins = pe.transpose(b_ps(f"SCOL{h}")[:, t:t + 1], scores[0:1, tok(4 * h + t)],
                                       ident[0:1, 0:1])
                ins.then_inc(b_full, 1)

            def b_ff(b, p):
                pe.wait_ge(m_free[p], T * (min(b + 2, NB) if isinstance(b, int) else b + 2) + 1)
                for t in range(2):
                    ins = sum_of(m_bank[p][:, D * t:D * (t + 1)],
                                 split_terms(lambda k, i: ct[:, k, i, tok(2 * p + t)],
                                             lambda k, j: wblk[:, j, k, :]))
                ins.then_inc(ff_full, 1)

            def turn(a, b, c):
                if c is not None:
                    b_s(c, 0)
                    b_s(c, 1)
                if b is not None:
                    a_moe(b, 0)
                if c is not None:
                    b_pt(c, 0)
                    b_s(c, 2)
                if b is not None:
                    a_moe(b, 1)
                if c is not None:
                    b_pt(c, 1)
                    b_s(c, 3)
                if a is not None:
                    a_gram(a, 0)
                if c is not None:
                    b_pt(c, 2)
                if a is not None:
                    a_gram(a, 1)
                if c is not None:
                    b_pt(c, 3)
                    b_o(c, 0)
                    b_o(c, 1)
                    b_o(c, 2)
                    b_o(c, 3)
                if b is not None:
                    a_moe(b, 2)
                if a is not None:
                    a_srow(a)
                if b is not None:
                    a_moe(b, 3)
                if c is not None:
                    b_pr(c, 0)
                    b_pr(c, 1)
                    b_pr(c, 2)
                    b_pr(c, 3)
                    b_tz(c, 0)
                if a is not None:
                    a_tx(a, 0)
                if c is not None:
                    b_tz(c, 1)
                if a is not None:
                    a_t(a, 0)
                if c is not None:
                    b_tz(c, 2)
                    b_tz(c, 3)
                if a is not None:
                    a_t(a, 1)
                if c is not None:
                    b_rout(c, 0)
                    b_rout(c, 1)
                    b_scol(c, 0)
                if a is not None:
                    a_trow(a)
                    a_tx(a, 1)
                if c is not None:
                    b_scol(c, 1)
                if b is not None:
                    a_moe(b, 4)
                if a is not None:
                    a_norm(a)
                if b is not None:
                    a_moe(b, 5)
                if a is not None:
                    a_g(a)
                if b is not None:
                    a_moe(b, 6)
                if a is not None:
                    a_iq(a)
                    a_csum(a)
                if b is not None:
                    b_tx(b, 0)
                if a is not None:
                    a_m(a)
                    a_tx(a, 2)
                if b is not None:
                    a_moe(b, 7)
                if a is not None:
                    a_cb(a)
                if c is not None:
                    b_ff(c, 0)
                    b_ff(c, 1)
                if a is not None:
                    a_tx(a, 3)
                if b is not None:
                    b_tx(b, 1)
                if a is not None:
                    a_ap(a, 0)
                if b is not None:
                    b_tx(b, 2)
                if c is not None:
                    b_ff(c, 2)
                    b_ff(c, 3)
                if a is not None:
                    a_ap(a, 1)
                if b is not None:
                    b_tx(b, 3)
                    b_f(b, 0)
                    b_f(b, 1)
                    b_f(b, 2)
                    b_f(b, 3)
                if a is not None:
                    a_ty(a, 0)
                if b is not None:
                    b_f(b, 4)
                    b_f(b, 5)
                if a is not None:
                    a_ty(a, 1)
                    a_ap(a, 2)
                if b is not None:
                    b_f(b, 6)
                if a is not None:
                    a_ap(a, 3)
                if b is not None:
                    b_f(b, 7)
                    b_f(b, 8)
                if a is not None:
                    a_ty(a, 2)
                if b is not None:
                    b_f(b, 9)
                if a is not None:
                    a_ty(a, 3)
                if b is not None:
                    b_f(b, 10)
                if a is not None:
                    a_gate(a)
                if b is not None:
                    b_f(b, 11)
                if a is not None:
                    a_wt(a)
                    a_bias(a, 0)
                    a_bias(a, 1)
                    a_bias(a, 2)
                    a_bias(a, 3)

            turn(0, None, None)
            turn(1, 0, None)
            with pe.Fori(2, NB) as i:
                turn(i, i - 1, i - 2)
            turn(None, NB - 1, NB - 2)
            turn(None, None, NB - 1)


_OUT_SHAPE = (8, 1024, 256)


def kernel(**inputs):
    import numpy as _np
    import concourse.bacc as _bacc
    from concourse import mybir as _mybir
    from concourse.bass_utils import run_bass_kernel_spmd as _run

    a = {k: _np.asarray(v) for k, v in inputs.items()}
    D, HEADS, DH = 256, 16, 16
    wqkv = a["L1_attn_Wqkv"].reshape(HEADS, 3, DH, D).transpose(1, 0, 2, 3).reshape(3 * D, D)
    eye = _np.eye(128, dtype=_np.float32)
    consts = _np.concatenate([eye, _np.tril(_np.ones((128, 128), _np.float32), -1)], axis=1)
    laid = [
        ("x", a["L0_attn_x"]),
        ("wqk_t", _np.concatenate([a["L0_attn_Wq"].T, a["L0_attn_Wk"].T], axis=1)),
        ("bqk", _np.concatenate([a["L0_attn_bq"], a["L0_attn_bk"]])),
        ("wv", a["L0_attn_Wv"]),
        ("bv", a["L0_attn_bv"].reshape(2, 128).T),
        ("gamma", a["L0_attn_gamma"]),
        ("gate_w", a["L0_ffn_gate_w"]),
        ("gate_b", a["L0_ffn_gate_b"]),
        ("expert_w", a["L0_ffn_expert_w"].transpose(1, 0, 2).reshape(D, -1)),
        ("expert_b", a["L0_ffn_expert_b"]),
        ("wqkv_t", wqkv.T),
        ("wproj_t", a["L1_attn_Wproj"].T),
        ("bproj", a["L1_attn_bproj"]),
        ("w_router", a["L1_ffn_w_router"].reshape(2, 128).T),
        ("w_block", a["L1_ffn_w_block"]),
        ("consts", consts),
    ]
    nc = _bacc.Bacc("TRN2", target_bir_lowering=False, num_devices=1)
    arrays, args = {}, []
    for name, v in laid:
        v = _np.ascontiguousarray(v)
        arrays[f"in_{name}_dram"] = v
        args.append(nc.dram_tensor(f"in_{name}_dram", v.shape, _mybir.dt.from_np(v.dtype),
                                   kind="ExternalInput").ap())
    args.append(nc.dram_tensor("out_0_dram", _OUT_SHAPE, _mybir.dt.float32, kind="ExternalOutput").ap())
    args.append(nc.dram_tensor("scratch_qkv", (3 * D, 2048), _mybir.dt.float16, kind="Internal").ap())
    args.append(nc.dram_tensor("scratch_o", (HEADS, DH, 8, 256), _mybir.dt.float16, kind="Internal").ap())
    build_two_layer_postln(nc, *args)
    r = _run(nc, [arrays], core_ids=[0])
    return r.results[0]["out_0_dram"]
```
